# Optimizing a Trainium2 kernel written in Bass

```python
import numpy as np
import jax
import jax.numpy as jnp

def _softmax(x, axis=-1):
    return jax.nn.softmax(x, axis=axis)

def _gelu(x):
    return jax.nn.gelu(x, approximate=True)

def _silu(x):
    return jax.nn.silu(x)

def _sigmoid(x):
    return jax.nn.sigmoid(x)

def _layernorm(x, axis=-1, eps=1e-05):
    m = jnp.mean(x, axis=axis, keepdims=True)
    v = jnp.var(x, axis=axis, keepdims=True)
    return (x - m) / jnp.sqrt(v + eps)

def _scatter_add(tgt, idx, src, axis=0):
    return tgt.at[idx].add(src)

def _segment_sum(src, seg, n):
    return jax.ops.segment_sum(src, seg, n)
kernel_name = 'mk_decoder_preln_d1_seqx_r8_dca355'

def setup_inputs(seed: int=0):
    np.random.seed(seed)
    _w = jnp.asarray

    def _rec_inputs():
        import jax
        import jax.numpy as jnp
        _rk = jax.random.key(seed)
        x = 7.22e-05 + 1 * jax.random.normal(jax.random.fold_in(_rk, 1), (8, 128, 256), jnp.float32)
        _lenS = 128 - jax.random.randint(jax.random.fold_in(_rk, 7), (8,), 0, max(1, 128 // 4) + 1, jnp.int32)
        _lenS2 = 128 - jax.random.randint(jax.random.fold_in(_rk, 8), (8,), 0, max(1, 128 // 4) + 1, jnp.int32)
        _ctx_2048P = jax.random.normal(jax.random.fold_in(_rk, 11), (8, 16, 256), jnp.float32)
        _ctx_2048c = jax.random.dirichlet(jax.random.fold_in(_rk, 511), 0.3 * jnp.ones((16,), jnp.float32), (8, 128))
        _ctx_2048t = jnp.einsum('bsk,bkd->bsd', _ctx_2048c, _ctx_2048P)
        _ctx_2048t = _ctx_2048t * jax.lax.rsqrt(jnp.mean(jnp.square(_ctx_2048t)) + 1e-12) * 0.953939
        ctx_2048 = 4.13588e-05 + 0.999923 * (_ctx_2048t + 0.3 * jax.random.normal(jax.random.fold_in(_rk, 611), (8, 128, 256), jnp.float32))
        _validS = jnp.arange(128)[None, :] < _lenS[:, None]
        _validS2 = jnp.arange(128)[None, :] < _lenS2[:, None]
        _causal = jnp.tril(jnp.ones((128, 128), dtype=bool))
        mask_1x1x2048x2048_if1 = jnp.where(jnp.ones((1, 1, 256, 256), dtype=bool), 1, 0).astype(jnp.int32)
        return (x, ctx_2048, mask_1x1x2048x2048_if1)
    x, ctx_2048, mask_1x1x2048x2048_if1 = _rec_inputs()

    def _L0_attn_setup():
        import jax, jax.numpy as jnp
        import numpy as np
        HIDDEN = 256
        NUM_HEADS = 32
        HEAD_DIM = 64
        NUM_KV = 8
        GROUP = NUM_HEADS // NUM_KV
        SCALE = HEAD_DIM ** (-0.5)
        ROPE_BASE = 10000.0

        def apply_rope(t):
            S, D = (t.shape[-2], t.shape[-1])
            inv_freq = 1.0 / ROPE_BASE ** (jnp.arange(0, D, 2, dtype=jnp.float32) / D)
            ang = jnp.arange(S, dtype=jnp.float32)[:, None] * inv_freq[None, :]
            cos, sin = (jnp.cos(ang), jnp.sin(ang))
            x1, x2 = (t[..., :D // 2], t[..., D // 2:])
            return jnp.concatenate([x1 * cos - x2 * sin, x2 * cos + x1 * sin], axis=-1)
        key = jax.random.key(seed)
        ks = jax.random.split(key, 10)
        B, S = (2, 256)
        s_in = HIDDEN ** (-0.5)
        s_o = (NUM_HEADS * HEAD_DIM) ** (-0.5)
        return {'x': jax.random.normal(ks[0], (B, S, HIDDEN), jnp.float32), 'Wq': jax.random.normal(ks[1], (NUM_HEADS * HEAD_DIM, HIDDEN), jnp.float32) * s_in, 'bq': jnp.zeros((NUM_HEADS * HEAD_DIM,), jnp.float32), 'Wk': jax.random.normal(ks[2], (NUM_KV * HEAD_DIM, HIDDEN), jnp.float32) * s_in, 'bk': jnp.zeros((NUM_KV * HEAD_DIM,), jnp.float32), 'Wv': jax.random.normal(ks[3], (NUM_KV * HEAD_DIM, HIDDEN), jnp.float32) * s_in, 'bv': jnp.zeros((NUM_KV * HEAD_DIM,), jnp.float32), 'Wo': jax.random.normal(ks[4], (HIDDEN, NUM_HEADS * HEAD_DIM), jnp.float32) * s_o, 'bo': jnp.zeros((HIDDEN,), jnp.float32), 'key_weights': jax.random.normal(ks[5], (NUM_HEADS,), jnp.float32)}
    _L0_attn_all = _L0_attn_setup()
    _L0_attn_in = {k: v for k, v in _L0_attn_all.items() if k in ('Wq', 'bq', 'Wk', 'bk', 'Wv', 'bv', 'Wo', 'bo', 'key_weights')}
    del _L0_attn_all

    def _L0_xattn_setup():
        import jax, jax.numpy as jnp
        import numpy as np
        import math
        CHANNELS = 128
        N_HEADS = 16
        K_CHANNELS = CHANNELS // N_HEADS
        ROPE_D = int(K_CHANNELS * 0.5)
        B, T = (4, 256)

        def apply_rope(x, d, base=10000.0):
            t = x.shape[2]
            theta = 1.0 / base ** (jnp.arange(0, d, 2, dtype=jnp.float32) / d)
            idx_theta = jnp.arange(t, dtype=jnp.float32)[:, None] * theta[None, :]
            idx_theta2 = jnp.concatenate([idx_theta, idx_theta], axis=-1)
            cos = jnp.cos(idx_theta2)[None, None, :, :]
            sin = jnp.sin(idx_theta2)[None, None, :, :]
            x_rope, x_pass = (x[..., :d], x[..., d:])
            d2 = d // 2
            neg_half = jnp.concatenate([-x_rope[..., d2:], x_rope[..., :d2]], axis=-1)
            x_rope = x_rope * cos + neg_half * sin
            return jnp.concatenate([x_rope, x_pass], axis=-1)
        key = jax.random.key(seed)
        ks = jax.random.split(key, 12)
        xavier = math.sqrt(6.0 / (CHANNELS + CHANNELS))
        inp = {'x': jax.random.normal(ks[0], (B, CHANNELS, T), dtype=jnp.float32), 'c': jax.random.normal(ks[1], (B, CHANNELS, T), dtype=jnp.float32), 'attn_mask': jnp.ones((1, 1, T, T), dtype=jnp.int32), 'wq': jax.random.uniform(ks[2], (CHANNELS, CHANNELS), jnp.float32, -xavier, xavier), 'bq': jnp.zeros((CHANNELS,), jnp.float32), 'wk': jax.random.uniform(ks[3], (CHANNELS, CHANNELS), jnp.float32, -xavier, xavier), 'bk': jnp.zeros((CHANNELS,), jnp.float32), 'wv': jax.random.uniform(ks[4], (CHANNELS, CHANNELS), jnp.float32, -xavier, xavier), 'bv': jnp.zeros((CHANNELS,), jnp.float32), 'wo': jax.random.normal(ks[5], (CHANNELS, CHANNELS), jnp.float32) * (1.0 / math.sqrt(CHANNELS)), 'bo': jnp.zeros((CHANNELS,), jnp.float32)}
        return inp
    _L0_xattn_all = _L0_xattn_setup()
    _L0_xattn_in = {k: v for k, v in _L0_xattn_all.items() if k in ('wq', 'bq', 'wk', 'bk', 'wv', 'bv', 'wo', 'bo')}
    del _L0_xattn_all

    def _L0_ffn_setup():
        import jax, jax.numpy as jnp
        import numpy as np
        D_MODEL = 256
        D_EXPERT = 1024
        EPS = 1e-08

        def ternary_quant(w):
            scale = jnp.mean(jnp.abs(w)) + EPS
            q = jnp.clip(jnp.round(w / scale), -1.0, 1.0) * scale
            return w + jax.lax.stop_gradient(q - w)
        key = jax.random.key(seed)
        k_x, k_up, k_gate, k_down = jax.random.split(key, 4)
        std_in = 1.0 / np.sqrt(D_MODEL)
        std_exp = 1.0 / np.sqrt(D_EXPERT)
        return {'x': jax.random.normal(k_x, (4, 256, D_MODEL), dtype=jnp.float32), 'W_up': jax.random.normal(k_up, (D_EXPERT, D_MODEL), dtype=jnp.float32) * std_in, 'W_gate': jax.random.normal(k_gate, (D_EXPERT, D_MODEL), dtype=jnp.float32) * std_in, 'W_down': jax.random.normal(k_down, (D_MODEL, D_EXPERT), dtype=jnp.float32) * std_exp}
    _L0_ffn_all = _L0_ffn_setup()
    _L0_ffn_in = {k: v for k, v in _L0_ffn_all.items() if k in ('W_up', 'W_gate', 'W_down')}
    del _L0_ffn_all
    return {'x': x, 'ctx_2048': ctx_2048, 'mask_1x1x2048x2048_if1': mask_1x1x2048x2048_if1, 'L0_attn_Wq': _L0_attn_in['Wq'], 'L0_attn_bq': _L0_attn_in['bq'], 'L0_attn_Wk': _L0_attn_in['Wk'], 'L0_attn_bk': _L0_attn_in['bk'], 'L0_attn_Wv': _L0_attn_in['Wv'], 'L0_attn_bv': _L0_attn_in['bv'], 'L0_attn_Wo': _L0_attn_in['Wo'], 'L0_attn_bo': _L0_attn_in['bo'], 'L0_attn_key_weights': _L0_attn_in['key_weights'], 'L0_xattn_wq': _L0_xattn_in['wq'], 'L0_xattn_bq': _L0_xattn_in['bq'], 'L0_xattn_wk': _L0_xattn_in['wk'], 'L0_xattn_bk': _L0_xattn_in['bk'], 'L0_xattn_wv': _L0_xattn_in['wv'], 'L0_xattn_bv': _L0_xattn_in['bv'], 'L0_xattn_wo': _L0_xattn_in['wo'], 'L0_xattn_bo': _L0_xattn_in['bo'], 'L0_ffn_W_up': _L0_ffn_in['W_up'], 'L0_ffn_W_gate': _L0_ffn_in['W_gate'], 'L0_ffn_W_down': _L0_ffn_in['W_down']}

def reference(x, ctx_2048, mask_1x1x2048x2048_if1, L0_attn_Wq, L0_attn_bq, L0_attn_Wk, L0_attn_bk, L0_attn_Wv, L0_attn_bv, L0_attn_Wo, L0_attn_bo, L0_attn_key_weights, L0_xattn_wq, L0_xattn_bq, L0_xattn_wk, L0_xattn_bk, L0_xattn_wv, L0_xattn_bv, L0_xattn_wo, L0_xattn_bo, L0_ffn_W_up, L0_ffn_W_gate, L0_ffn_W_down):
    import jax
    import jax.numpy as jnp

    def _L0_attn_ref(x, Wq, bq, Wk, bk, Wv, bv, Wo, bo, key_weights):
        import jax, jax.numpy as jnp
        import numpy as np
        HIDDEN = 256
        NUM_HEADS = 32
        HEAD_DIM = 64
        NUM_KV = 8
        GROUP = NUM_HEADS // NUM_KV
        SCALE = HEAD_DIM ** (-0.5)
        ROPE_BASE = 10000.0

        def apply_rope(t):
            S, D = (t.shape[-2], t.shape[-1])
            inv_freq = 1.0 / ROPE_BASE ** (jnp.arange(0, D, 2, dtype=jnp.float32) / D)
            ang = jnp.arange(S, dtype=jnp.float32)[:, None] * inv_freq[None, :]
            cos, sin = (jnp.cos(ang), jnp.sin(ang))
            x1, x2 = (t[..., :D // 2], t[..., D // 2:])
            return jnp.concatenate([x1 * cos - x2 * sin, x2 * cos + x1 * sin], axis=-1)
        B, S, _ = x.shape
        q = (x @ Wq.T + bq).reshape(B, S, NUM_HEADS, HEAD_DIM).transpose(0, 2, 1, 3)
        k = (x @ Wk.T + bk).reshape(B, S, NUM_KV, HEAD_DIM).transpose(0, 2, 1, 3)
        v = (x @ Wv.T + bv).reshape(B, S, NUM_KV, HEAD_DIM).transpose(0, 2, 1, 3)
        q = apply_rope(q)
        k = apply_rope(k)
        qg = q.reshape(B, NUM_KV, GROUP, S, HEAD_DIM)
        scores = jnp.einsum('bkgsd,bktd->bkgst', qg, k) * SCALE
        scores = scores * key_weights.reshape(1, NUM_KV, GROUP, 1, 1)
        causal = jnp.tril(jnp.ones((S, S), bool))
        scores = jnp.where(causal, scores, -jnp.inf)
        a = jax.nn.softmax(scores, axis=-1)
        o = jnp.einsum('bkgst,bktd->bkgsd', a, v)
        o = o.reshape(B, NUM_HEADS, S, HEAD_DIM).transpose(0, 2, 1, 3).reshape(B, S, NUM_HEADS * HEAD_DIM)
        return o @ Wo.T + bo

    def _L0_xattn_ref(x, c, attn_mask, wq, bq, wk, bk, wv, bv, wo, bo):
        import jax, jax.numpy as jnp
        import numpy as np
        import math
        CHANNELS = 128
        N_HEADS = 16
        K_CHANNELS = CHANNELS // N_HEADS
        ROPE_D = int(K_CHANNELS * 0.5)
        B, T = (4, 256)

        def apply_rope(x, d, base=10000.0):
            t = x.shape[2]
            theta = 1.0 / base ** (jnp.arange(0, d, 2, dtype=jnp.float32) / d)
            idx_theta = jnp.arange(t, dtype=jnp.float32)[:, None] * theta[None, :]
            idx_theta2 = jnp.concatenate([idx_theta, idx_theta], axis=-1)
            cos = jnp.cos(idx_theta2)[None, None, :, :]
            sin = jnp.sin(idx_theta2)[None, None, :, :]
            x_rope, x_pass = (x[..., :d], x[..., d:])
            d2 = d // 2
            neg_half = jnp.concatenate([-x_rope[..., d2:], x_rope[..., :d2]], axis=-1)
            x_rope = x_rope * cos + neg_half * sin
            return jnp.concatenate([x_rope, x_pass], axis=-1)
        b, _, t_t = x.shape
        t_s = c.shape[2]
        q = jnp.einsum('oi,bit->bot', wq, x) + bq[None, :, None]
        k = jnp.einsum('oi,bit->bot', wk, c) + bk[None, :, None]
        v = jnp.einsum('oi,bit->bot', wv, c) + bv[None, :, None]

        def split_heads(z, t):
            return z.reshape(b, N_HEADS, K_CHANNELS, t).transpose(0, 1, 3, 2)
        q = split_heads(q, t_t)
        k = split_heads(k, t_s)
        v = split_heads(v, t_s)
        q = apply_rope(q, ROPE_D)
        k = apply_rope(k, ROPE_D)
        scores = jnp.einsum('bhqc,bhkc->bhqk', q, k) / math.sqrt(K_CHANNELS)
        scores = jnp.where(attn_mask == 0, jnp.float32(-10000.0), scores)
        p_attn = jax.nn.softmax(scores, axis=-1)
        out = jnp.einsum('bhqk,bhkc->bhqc', p_attn, v)
        out = out.transpose(0, 1, 3, 2).reshape(b, CHANNELS, t_t)
        out = jnp.einsum('oi,bit->bot', wo, out) + bo[None, :, None]
        return out

    def _L0_ffn_ref(x, W_up, W_gate, W_down):
        import jax, jax.numpy as jnp
        import numpy as np
        D_MODEL = 256
        D_EXPERT = 1024
        EPS = 1e-08

        def ternary_quant(w):
            scale = jnp.mean(jnp.abs(w)) + EPS
            q = jnp.clip(jnp.round(w / scale), -1.0, 1.0) * scale
            return w + jax.lax.stop_gradient(q - w)
        wu = ternary_quant(W_up)
        wg = ternary_quant(W_gate)
        wd = ternary_quant(W_down)
        up = jnp.einsum('bsd,ed->bse', x, wu)
        gate = jnp.einsum('bsd,ed->bse', x, wg)
        hidden = jax.nn.silu(up) * gate
        return jnp.einsum('bse,de->bsd', hidden, wd)
    x = x + _L0_attn_ref(_layernorm(x, axis=-1), L0_attn_Wq, L0_attn_bq, L0_attn_Wk, L0_attn_bk, L0_attn_Wv, L0_attn_bv, L0_attn_Wo, L0_attn_bo, L0_attn_key_weights)
    x = x + _L0_xattn_ref(_layernorm(x, axis=-1), ctx_2048, mask_1x1x2048x2048_if1, L0_xattn_wq, L0_xattn_bq, L0_xattn_wk, L0_xattn_bk, L0_xattn_wv, L0_xattn_bv, L0_xattn_wo, L0_xattn_bo)
    x = x + _L0_ffn_ref(_layernorm(x, axis=-1), L0_ffn_W_up, L0_ffn_W_gate, L0_ffn_W_down)
    return x

_drawn_inputs = setup_inputs


def setup_inputs(seed=0):
    import zlib

    import numpy as np

    out = dict(_drawn_inputs(seed))
    spreads = {'L0_attn_bq': (0.0, 0.327),
     'L0_attn_bk': (0.0, 0.559),
     'L0_attn_bv': (0.0, 0.1),
     'L0_attn_bo': (0.0, 0.1),
     'L0_xattn_bq': (0.0, 0.303),
     'L0_xattn_bk': (0.0, 0.8),
     'L0_xattn_bv': (0.0, 0.1),
     'L0_xattn_bo': (0.0, 0.1)}
    factors = {}
    for name, (base, spread) in spreads.items():
        noise = np.random.default_rng([zlib.crc32(name.encode()), seed]).standard_normal(out[name].shape)
        drawn = base * np.exp(spread * noise) if base else spread * noise
        out[name] = jnp.asarray(drawn.astype(out[name].dtype))
    for name, factor in factors.items():
        out[name] = (out[name] * factor).astype(out[name].dtype)
    return out
```

```python
from contextlib import ExitStack

import numpy as np
import concourse.bass as bass
from concourse import mybir

F32 = mybir.dt.float32
F16 = mybir.dt.float16
BF16 = mybir.dt.bfloat16
I32 = mybir.dt.int32
ALU = mybir.AluOpType
ACT = mybir.ActivationFunctionType
AX = mybir.AxisListType

B, S, D = 8, 128, 256
P = 128
KD = D // P
NH, NKV, HD = 32, 8, 64
GRP = NH // NKV
NPAIR = NKV // 2
XH, XC, XG = 16, 8, 4
XJ = XH // XG
T = D
TB = T // P
E = 1024
ET = E // P
BIG = 1.0e30
MROW, MSCALE = 24, 256.0
HS = 1.0 / 32
EPS_LN, EPS_Q = 1e-5, 1e-8
HUGE = 2.0 ** 100

C32 = {}
_at = 0
for _n, _w in (("ident", P), ("causal", P), ("cos", HD), ("sin", HD), ("xk_cos", T), ("xk_sin", T),
               ("xq_cos", T), ("xq_sin", T), ("kcol", 1), ("selsum", P)):
    C32[_n] = (_at, _at + _w)
    _at += _w
W32 = _at
C16 = {"ident": (0, P), "ten": (P, 2 * P), "k_hi": (256, 768), "k_lo": (768, 1280), "q_hi": (1280, 1792), "q_lo": (1792, 2304)}
W16 = 2304
NQKV = (NH + 2 * NKV) * HD
R_K, R_V, R_Q = 0, NKV * HD, 2 * NKV * HD
R_BO, R_XBV, R_KW = NQKV, NQKV + D, NQKV + D + P
WROW = NQKV + D + P + NH

SELF_SIGNALS = dict(
    ln1=3, rstd1=1, xn1=1, xres=1, xnT_ps=1, xnT=1,
    qkv_ps=6, rope_mul=10, rope_sum=5, roped=5, hi=5, lo=5, kswap=1, v_sb=1,
    qkT_ps=6, qkT=6, s_ps=8, masked=32, expd=32, rsum=8, normed=8, pT_ps=8, pT=8, pv=8, oT=4, o_ps=1, x1=1)
REST_SIGNALS = dict(
    ln2=3, rstd2=1, xn2=1, xproj=3, xr_mul=4, xr_sum=2, xr_hi=2, xr_lo=2, xv=1, sel_ps=4, kst=2, qst=2, kz=4,
    nat_ps=16, xmax=16, mt=1, mt_ps=1, mrow=1, qaug=1, st_ps=16, xexp=16, xpv=16, oraw=4, bc_ps=4, bc=4, onorm=4,
    wo_ps=1, x2=1, ln3=3, rstd3=1, xn3=1, x3T_ps=1, x3h=1, x3l=1,
    ff_ps=4, ftanh=2, fact=2, fhid=2, fh=2, fl=2, dn_ps=1, outt=1)

CHUNKS = ["k", "v", "q0", "q1", "q2", "q3"]
ROPED = ["k", "q0", "q1", "q2", "q3"]


def self_order():
    o = [("ln", 0), ("qkv", 0), ("qkv", 1), ("qkv", 2), ("split", 0), ("qkv", 3), ("split", 1), ("tr", 0), ("tr", 1),
         ("qkv", 4), ("split", 2), ("tr", 2), ("qkv", 5), ("split", 3), ("tr", 3), ("split", 4), ("tr", 4), ("tr", 5)]
    o += [("s", 0), ("s", 1)]
    for g in range(NKV):
        o.append(("p", g))
        if g + 2 < NKV:
            o.append(("s", g + 2))
    return o + [("o", 0)]


def rest_order():
    o = [("ln2", 0), ("proj", 0), ("proj", 1), ("rope", 0), ("rope", 1), ("sel", 0), ("sel", 1), ("kz", 0)]
    o += [("nat", h) for h in range(XH)] + [("m", 0), ("st", 0), ("st", 1)]
    for h in range(XH):
        o.append(("pv", h))
        if h + 2 < XH:
            o.append(("st", h + 2))
        if h % XJ == 1 and h > XJ:
            o.append(("nrm", h // XJ - 1))
    return o + [("nrm", XG - 1), ("wo", 0), ("ln3", 0), ("t3", 0), ("ff", 0), ("ff", 1), ("down", 0)]


COST = {"ln": 1.0, "qkv": 3.0, "split": 0.5, "tr": 0.8, "s": 1.5, "p": 2.0, "o": 7.0,
        "ln2": 1.0, "proj": 1.0, "rope": 0.7, "sel": 0.5, "kz": 0.3, "nat": 0.6, "m": 1.0, "st": 0.6, "pv": 0.6,
        "nrm": 0.7, "wo": 2.0, "ln3": 1.0, "t3": 0.5, "ff": 2.5, "down": 2.0}


def merged(a, b):
    ta, tb = sum(COST[n] for n, _ in a), sum(COST[n] for n, _ in b)
    out, i, j, ca, cb = [], 0, 0, 0.0, 0.0
    while i < len(a) or j < len(b):
        hold = i < len(a) and a[i][0] == "o" and ("wo", 0) in b[j:]
        if j >= len(b) or (i < len(a) and not hold and ca / ta <= cb / tb):
            out.append(("self",) + a[i])
            ca += COST[a[i][0]]
            i += 1
        else:
            out.append(("rest",) + b[j])
            cb += COST[b[j][0]]
            j += 1
    return out


def build(nc, x, ctx, mask_n, mask_t, w_qkv, w_o, rows, cols, xw, xwo, w_up, w_gate, w_down, c32, c16, out):
    with ExitStack() as st:
        def sb(name, shape, dt=F32):
            return st.enter_context(nc.sbuf_tensor(name, shape, dt))

        def sem(name):
            return st.enter_context(nc.semaphore(name))

        k32 = sb("k32", [P, W32])
        k16 = sb("k16", [P, W16], F16)
        rowb = sb("rowb", [P, WROW])
        colb = sb("colb", [P, 5])
        wqkv = sb("wqkv", [P, KD, NQKV])
        wo = sb("wo", [P, NPAIR, GRP, D])
        xw_sb = sb("xw_sb", [P, 5, P])
        xwo_sb = sb("xwo_sb", [P, XG, P])
        ffw = sb("ffw", [P, 3, KD * E])
        tern = sb("tern", [P, 3, KD * E], F16)
        cq = sb("cq", [P, NH, HD])
        sq = sb("sq", [P, NH, HD])
        maskn = ffw[:, 0, 0:512].bitcast(I32)
        maskt = ffw[:, 0, 512:1024].bitcast(I32)
        nbn = sb("nbn", [P, TB, T], F16)
        nbt = sb("nbt", [P, TB, T], F16)
        bigi = sb("bigi", [P, 2, P], BF16)
        small = sb("small", [P, 32])
        flag = sb("flag", [P, 1], I32)
        half = sb("half", [P, 1])
        ones = sb("ones", [P, P])
        ident = k32[:, C32["ident"][0]:C32["ident"][1]]
        ident16 = k16[:, 0:P]

        def c(name):
            return k32[:, C32[name][0]:C32[name][1]]

        x_sb = sb("x_sb", [P, D])
        xres = sb("xres", [P, D])
        xn1 = sb("xn1", [P, D])
        xnT = sb("xnT", [P, KD, P])
        st1, mv1, rs1 = sb("st1", [P, 6]), sb("mv1", [P, 3]), sb("rs1", [P, 1])
        rot_b = sb("rot_b", [P, 512])
        rot = sb("rot", [P, 2, 512])
        qs = sb("qs", [P, 2, 8, 2, HD], F16)
        ks = sb("ks", [P, NKV, 2, 2, HD], F16)
        v_sb = sb("v_sb", [P, NKV * HD])
        qT = sb("qT", [P, NH, P], F16)
        kT = sb("kT", [P, NKV, 2, P], F16)
        sm = sb("sm", [P, 2, GRP, P])
        ex = sb("ex", [P, 2, GRP, P])
        nmax = sb("nmax", [P, NH])
        ssum = sb("ssum", [P, NH])
        rinv = sb("rinv", [P, NH])
        pT = sb("pT", [P, 2, GRP * P])
        oT = sb("oT", [P, NPAIR, GRP, P])
        x1 = sb("x1", [P, D])
        ctx_sb = sb("ctx_sb", [P, D])
        xn2 = sb("xn2", [P, T])
        st2, mv2, rs2 = sb("st2", [P, 6]), sb("mv2", [P, 3]), sb("rs2", [P, 1])
        xr_a = sb("xr_a", [P, T])
        xr_b = sb("xr_b", [P, T])
        xr = sb("xr", [P, 2, T])
        xhl = sb("xhl", [P, 2, 2, T], F16)
        kst = sb("kst", [P, XG, T], F16)
        qst = sb("qst", [P, XG, T], F16)
        mrow = kst
        qaug = sb("qaug", [P, XG, T], F16)
        kz = sb("kz", [P, XG, XJ, T], F16)
        vaug = sb("vaug", [P, TB, XH, 32])
        xnm = sb("xnm", [P, XG, XJ, TB])
        mt = sb("mt", [P, TB, XG, P], F16)
        xpT = ffw[:, 0, 0:1024].rearrange("p (n m t) -> p n m t", n=2, m=TB)
        oraw = ffw[:, 0, 1024:2048].rearrange("p (g t) -> p g t", g=XG)
        bcs = ffw[:, 2, 0:512].rearrange("p (n t) -> p n t", n=2)
        x2 = ffw[:, 2, 512:768]
        xn3 = ffw[:, 2, 768:1024]
        st3, mv3, rs3 = sb("st3", [P, 6]), sb("mv3", [P, 3]), sb("rs3", [P, 1])
        x3 = ffw[:, 2, 1024:1280].bitcast(F16).rearrange("p (v k s) -> p v k s", v=2, k=KD)
        fe = ffw[:, 1, 0:1024].rearrange("p (f n) -> p f n", f=2)
        hid = ffw[:, 1, 1024:2048].bitcast(F16).rearrange("p (v e s) -> p v e s", v=2, e=ET)
        outt = ffw[:, 2, 1280:1536]

        PS = st.enter_context(nc.psum_tensor("PS", [P, 8, 512], F32))
        A = [PS[:, n, :] for n in range(4)]
        Bk = [PS[:, n, :] for n in range(4, 8)]

        sg = {n: sem(n) for n in (*SELF_SIGNALS, *REST_SIGNALS)}
        per = {**SELF_SIGNALS, **REST_SIGNALS}
        x_in, ctx_in, out_st, out_free = sem("x_in"), sem("ctx_in"), sem("out_st"), sem("out_free")
        d_const, d_row, d_wkv, d_wq, d_wo, d_x, d_mask = (sem(n) for n in ("d_const", "d_row", "d_wkv", "d_wq", "d_wo", "d_xw", "d_mask"))
        d_ffw = [sem(f"d_ffw{n}") for n in range(3)]
        tabs, rbs, zeroed, nbs, ffsum, totals, scales, terns, pool_set, flagged = (
            sem(n) for n in ("tabs", "rbs", "zeroed", "nbs", "ffsum", "totals", "scales", "terns", "pool_set", "flagged"))
        passed = sem("passed")

        def wait(eng, name, b, k):
            v = b * per[name] + k
            if not (type(v) is int and v <= 0):
                eng.wait_ge(sg[name], v)

        block = st.enter_context(nc.Block())

        def batches(eng, selfs, rests):
            for n, k in self_order():
                selfs[n](0, k)
            with eng.Fori(1, B) as i:
                for chain, n, k in merged(self_order(), rest_order()):
                    if chain == "self":
                        selfs[n](i, k)
                    else:
                        rests[n](i - 1, k)
            for n, k in rest_order():
                rests[n](B - 1, k)

        @block.sync
        def _(sp):
            sp.sem_inc(out_free, 1)
            sp.dma_start(x_sb[:], x[0]).then_inc(x_in, 16)
            sp.dma_start(k32[:], c32).then_inc(d_const, 16)
            sp.dma_start(wqkv[:, :, 0:2 * NKV * HD], w_qkv[:, :, 0:2 * NKV * HD]).then_inc(d_wkv, 16)
            sp.dma_start(wqkv[:, :, 2 * NKV * HD:], w_qkv[:, :, 2 * NKV * HD:]).then_inc(d_wq, 16)
            sp.dma_start(ctx_sb[:], ctx[0]).then_inc(ctx_in, 16)
            sp.dma_start(wo[:], w_o).then_inc(d_wo, 16)
            sp.wait_ge(sg["xn1"], 1)
            sp.wait_ge(sg["xres"], 1)
            sp.dma_start(x_sb[:], x[1]).then_inc(x_in, 16)

            def ahead(b):
                if not (type(b) is int and b == B - 1):
                    sp.wait_ge(sg["xn1"], b + 1)
                    sp.wait_ge(sg["xres"], b + 1)
                    src = x[b + 1] if type(b) is int else x[bass.ds(b + 1, 1)].rearrange("a p n -> (a p) n")
                    sp.dma_start(x_sb[:], src).then_inc(x_in, 16)
                sp.wait_ge(sg["xproj"], (b - 1) * 3 + 2)
                src = ctx[b] if type(b) is int else ctx[bass.ds(b, 1)].rearrange("a p n -> (a p) n")
                sp.dma_start(ctx_sb[:], src).then_inc(ctx_in, 16)
                store(b - 1)

            def store(b):
                sp.wait_ge(sg["outt"], b + 1)
                dst = out[b] if type(b) is int else out[bass.ds(b, 1)].rearrange("a p n -> (a p) n")
                sp.dma_start(dst, outt[:]).then_inc(out_st, 16)
                sp.wait_ge(out_st, b * 16 + 16)
                sp.sem_inc(out_free, 1)

            with sp.Fori(1, B - 1) as i:
                ahead(i)
            ahead(B - 1)
            store(B - 1)

        @block.tensor
        def _(pe):
            mm = nc.tensor.matmul

            pe.wait_ge(zeroed, 1)
            pe.wait_ge(ffsum, 4)
            mm(Bk[0][:, 0:4], ones[:], small[:, 0:4], start=True, stop=True).then_inc(totals, 1)
            pe.wait_ge(d_const, 32)

            pe.wait_ge(flagged, 1)
            any_masked = pe.value_load(flag[0:1, 0:1])
            pe.wait_ge(nbs, 4)

            def masked(dst, hidden, stop):
                mm(dst, bigi[:, 0, :], hidden, start=False, stop=False)
                mm(dst, bigi[:, 1, :], hidden, start=False, stop=False)
                return mm(dst, k16[:, P:2 * P], hidden, start=False, stop=stop)

            def s_ln(b, _):
                wait(pe, "xn1", b, 1)
                if type(b) is not int:
                    wait(pe, "pT", b - 1, 8)
                for k in range(KD):
                    last = nc.tensor.transpose(A[2][:, k * P:(k + 1) * P], xn1[:, k * P:(k + 1) * P], ident)
                last.then_inc(sg["xnT_ps"], 1)

            def s_qkv(b, n):
                if n == 0:
                    wait(pe, "xnT", b, 1)
                    wait(pe, "x1", b - 1, 1) if type(b) is not int else None
                    pe.wait_ge(d_wkv, 16)
                if n == 1:
                    wait(pe, "masked", b, 0)
                if n == 2:
                    pe.wait_ge(d_wq, 16)
                if n >= 2:
                    if n == 3:
                        wait(pe, "v_sb", b, 1)
                    else:
                        wait(pe, "rope_mul", b, {2: 2, 4: 4, 5: 6}[n])
                for k in range(KD):
                    last = mm(A[n % 2], xnT[:, k, :], wqkv[:, k, n * 512:(n + 1) * 512], start=(k == 0), stop=(k == KD - 1))
                last.then_inc(sg["qkv_ps"], 1)

            def s_tr(b, n):
                if n < 2:
                    wait(pe, "kswap", b, 1)
                    src = [ks[:, g, v] for g in range(4 * n, 4 * n + 4) for v in range(2)]
                else:
                    wait(pe, "lo", b, n)
                    src = [qs[:, n % 2, h] for h in range(8)]
                wait(pe, "qkT", b, n) if n else wait(pe, "xnT", b, 1)
                dst = A[2].bitcast(F16)
                for m, a in enumerate(src):
                    last = nc.tensor.transpose(dst[:, m * P:(m + 1) * P], a.rearrange("p t d -> p (t d)"), ident16)
                last.then_inc(sg["qkT_ps"], 1)

            def s_s(b, g):
                wait(pe, "qkT", b, 3 + g // 2)
                if g >= 2:
                    wait(pe, "masked", b, 4 * (g - 1))
                elif g == 0:
                    wait(pe, "rope_mul", b, 10)
                for j in range(GRP):
                    for v in range(2):
                        last = mm(A[g % 2][:, j * P:(j + 1) * P], qT[:, GRP * g + j, :], kT[:, g, v, :],
                                  start=(v == 0), stop=(v == 1))
                last.then_inc(sg["s_ps"], 1)

            def s_p(b, g):
                wait(pe, "normed", b, g + 1)
                wait(pe, "pT", b, g) if g else wait(pe, "qkT", b, 6)
                for j in range(GRP):
                    last = nc.tensor.transpose(A[2][:, j * P:(j + 1) * P], ex[:, g % 2, j, :], ident)
                last.then_inc(sg["pT_ps"], 1)
                if g == 0:
                    wait(pe, "v_sb", b, 1)
                if g % 2 == 0 and g:
                    wait(pe, "oT", b, g // 2)
                wait(pe, "pT", b, g + 1)
                e = g % 2
                mm(A[3][HD * e:HD * e + HD, :], v_sb[:, g * HD:(g + 1) * HD], pT[:, g % 2, :],
                   start=True, stop=True).then_inc(sg["pv"], 1)

            def s_o(b, _):
                pe.wait_ge(d_wo, 16)
                wait(pe, "oT", b, NPAIR)
                wait(pe, "masked", b, NH)
                for n in range(NPAIR * GRP):
                    last = mm(A[0][:, 0:D], oT[:, n // GRP, n % GRP, :], wo[:, n // GRP, n % GRP, :],
                              start=(n == 0), stop=(n == NPAIR * GRP - 1))
                last.then_inc(sg["o_ps"], 1)

            def r_ln2(b, _):
                pass

            def r_proj(b, n):
                if n == 0:
                    pe.wait_ge(d_x, 32)
                    pe.wait_ge(ctx_in, b * 16 + 16)
                    for m in range(2):
                        last = mm(Bk[1][:, m * T:(m + 1) * T], xw_sb[:, 2 + m, :], ctx_sb[:], start=True, stop=True)
                    last.then_inc(sg["xproj"], 1)
                    for m in range(TB):
                        last = mm(Bk[2][:, m * P:(m + 1) * P], ctx_sb[:, m * P:(m + 1) * P], xw_sb[:, 4, :], start=True, stop=True)
                    last.then_inc(sg["xproj"], 1)
                else:
                    wait(pe, "xn2", b, 1)
                    for m in range(2):
                        last = mm(Bk[0][:, m * T:(m + 1) * T], xw_sb[:, m, :], xn2[:], start=True, stop=True)
                    last.then_inc(sg["xproj"], 1)

            def r_sel(b, n):
                wait(pe, "xr_lo", b, n + 1)
                hi, lo = (("k_hi", "k_lo"), ("q_hi", "q_lo"))[n]
                for m in range(2):
                    if n == 1 and m == 0:
                        wait(pe, "xr_mul", b, 4)
                    if n == 1 and m == 1:
                        wait(pe, "xv", b, 1)
                    dst = (Bk[3], Bk[1], Bk[0], Bk[2])[2 * n + m]
                    for q in range(2):
                        hg = 2 * m + q
                        for v, name in enumerate((hi, lo)):
                            at = C16[name][0] + hg * P
                            last = mm(dst[:, q * T:(q + 1) * T], k16[:, at:at + P], xhl[:, n, v, :], start=(v == 0), stop=(v == 1))
                    last.then_inc(sg["sel_ps"], 1)

            def r_kz(b, _):
                pass

            def r_nat(b, h):
                if h == 0:
                    wait(pe, "kz", b, XJ)
                    wait(pe, "qst", b, 2)
                if h >= 2:
                    wait(pe, "xmax", b, h - 1)
                def products(hide):
                    for m in range(TB):
                        dst = Bk[h % 2][:, m * T:(m + 1) * T]
                        last = mm(dst, qst[:, h // XJ, m * P:(m + 1) * P], kz[:, h // XJ, h % XJ, :], start=True, stop=not hide)
                        if hide:
                            last = masked(dst, nbn[:, m, :], True)
                    last.then_inc(sg["nat_ps"], 1)

                with pe.If(any_masked):
                    products(True)
                with pe.Else():
                    products(False)

            def r_m(b, _):
                wait(pe, "mt", b, 1)
                dst = Bk[2].bitcast(F16)
                for hg in range(XG):
                    for m in range(TB):
                        last = nc.tensor.transpose(dst[:, hg * T + m * P:hg * T + (m + 1) * P], mt[:, m, hg, :], ident16)
                last.then_inc(sg["mt_ps"], 1)

            def r_st(b, h):
                if h == 0:
                    wait(pe, "qaug", b, 1)
                if h >= 2:
                    wait(pe, "xexp", b, h - 1)
                def products(hide):
                    for m in range(TB):
                        dst = Bk[2 + h % 2][:, m * T:(m + 1) * T]
                        k = kz[:, h // XJ, h % XJ, m * P:(m + 1) * P]
                        if hide:
                            mm(dst, k, qst[:, h // XJ, :], start=True, stop=False)
                            masked(dst, nbt[:, m, :], False)
                            last = mm(dst, k, mrow[:, h // XJ, :], start=False, stop=True)
                        else:
                            last = mm(dst, k, qaug[:, h // XJ, :], start=True, stop=True)
                    last.then_inc(sg["st_ps"], 1)

                with pe.If(any_masked):
                    products(True)
                with pe.Else():
                    products(False)

            def r_pv(b, h):
                hg, j = h // XJ, h % XJ
                wait(pe, "xexp", b, h + 1)
                if h == 0:
                    wait(pe, "xmax", b, XH)
                if j == 0 and hg >= 2:
                    wait(pe, "bc", b, hg - 1)
                for m in range(TB):
                    last = mm(Bk[hg % 2][32 * j:32 * j + 32, 0:T], vaug[:, m, h, :], xpT[:, h % 2, m, :],
                              start=(m == 0), stop=(m == TB - 1))
                last.then_inc(sg["xpv"], 1)

            def r_nrm(b, hg):
                wait(pe, "oraw", b, hg + 1)
                mm(Bk[hg % 2][:, T:2 * T], c("selsum"), oraw[:, hg, :], start=True, stop=True).then_inc(sg["bc_ps"], 1)

            def r_wo(b, _):
                wait(pe, "onorm", b, XG)
                for hg in range(XG):
                    last = mm(Bk[0][:, 0:T], xwo_sb[:, hg, :], oraw[:, hg, :], start=(hg == 0), stop=(hg == XG - 1))
                last.then_inc(sg["wo_ps"], 1)

            def r_ln3(b, _):
                pass

            def r_t3(b, _):
                wait(pe, "xn3", b, 1)
                for k in range(KD):
                    last = nc.tensor.transpose(Bk[1][:, k * P:(k + 1) * P], xn3[:, k * P:(k + 1) * P], ident)
                last.then_inc(sg["x3T_ps"], 1)

            def r_ff(b, f):
                if f == 0:
                    wait(pe, "x3l", b, 1)
                    pe.wait_ge(terns, 3)
                for w in range(2):
                    dst = (Bk[0], Bk[2], Bk[3], Bk[1])[2 * f + w]
                    for e in range(ET // 2):
                        at = (f * (ET // 2) + e) * P
                        for m in range(2 * KD):
                            k, v = m // 2, m % 2
                            last = mm(dst[:, e * P:(e + 1) * P], tern[:, w, k * E + at:k * E + at + P], x3[:, v, k, :],
                                      start=(m == 0), stop=(m == 2 * KD - 1))
                    last.then_inc(sg["ff_ps"], 1)

            def r_down(b, _):
                wait(pe, "fl", b, 2)
                for e in range(ET):
                    for v in range(2):
                        last = mm(Bk[0][:, 0:D], hid[:, v, e, :], tern[:, 2, e * D:(e + 1) * D],
                                  start=(e == 0 and v == 0), stop=(e == ET - 1 and v == 1))
                last.then_inc(sg["dn_ps"], 1)

            batches(pe, dict(ln=s_ln, qkv=s_qkv, split=lambda b, n: None, tr=s_tr, s=s_s, p=s_p, o=s_o),
                    dict(ln2=r_ln2, proj=r_proj, rope=lambda b, n: None, sel=r_sel, kz=r_kz, nat=r_nat, m=r_m, st=r_st, pv=r_pv,
                         nrm=r_nrm, wo=r_wo, ln3=r_ln3, t3=r_t3, ff=r_ff, down=r_down))

        @block.vector
        def _(dve):
            v = nc.vector

            v.memset(ones[:], 1.0).then_inc(zeroed, 1)
            v.memset(half[:], -0.5).then_inc(pool_set, 1)

            def layernorm(b, src, stt, mv, rs, dst, n, ready):
                ln, rstd, xn = f"ln{n}", f"rstd{n}", f"xn{n}"
                ready()
                v.bn_stats(stt[:], src[:]).then_inc(sg[ln], 1)
                wait(dve, ln, b, 1)
                dve.sem_inc(passed, 1)
                v.bn_aggr(mv[:, 0:2], stt[:]).then_inc(sg[ln], 1)
                wait(dve, ln, b, 2)
                v.tensor_scalar(mv[:, 2:3], mv[:, 1:2], EPS_LN, None, ALU.add).then_inc(sg[ln], 1)
                wait(dve, rstd, b, 1)
                v.tensor_scalar(dst[:], src[:], mv[:, 0:1], rs[:], ALU.subtract, ALU.mult).then_inc(sg[xn], 1)

            def s_ln(b, _):
                layernorm(b, x_sb, st1, mv1, rs1, xn1, 1, lambda: dve.wait_ge(x_in, b * 16 + 16))

            def tables(r):
                if r == 0:
                    return (c("cos").rearrange("p (o d) -> p o d", o=1).to_broadcast([P, 8, HD]),
                            c("sin").rearrange("p (o d) -> p o d", o=1).to_broadcast([P, 8, HD]))
                return cq[:, 8 * (r - 1):8 * r, :], sq[:, 8 * (r - 1):8 * r, :]

            def rotate(r, src, dst):
                cos, sin = tables(r)
                yield v.tensor_tensor(dst.rearrange("p (h d) -> p h d", d=HD), src.rearrange("p (h d) -> p h d", d=HD), cos, ALU.mult)
                yield v.tensor_tensor(rot_b[:].rearrange("p (h t d) -> p h t d", t=2, d=HD // 2),
                                      src.rearrange("p (h t d) -> p h t d", t=2, d=HD // 2)[:, :, ::-1, :],
                                      sin.rearrange("p h (t d) -> p h t d", t=2), ALU.mult)

            def s_qkv(b, n):
                wait(dve, "qkv_ps", b, n + 1)
                if n == 1:
                    v.tensor_tensor(v_sb[:], A[1], rowb[:, R_V:R_V + 512], ALU.add).then_inc(sg["v_sb"], 1)
                    return
                r = max(0, n - 1)
                if r:
                    wait(dve, "rope_sum", b, r)
                if r >= 2:
                    wait(dve, "lo", b, r - 1)
                for ins in rotate(r, A[n % 2], rot[:, r % 2, :]):
                    ins.then_inc(sg["rope_mul"], 1)
                wait(dve, "rope_mul", b, 2 * r + 2)
                v.tensor_tensor(rot[:, r % 2, :], rot[:, r % 2, :], rot_b[:], ALU.add).then_inc(sg["rope_sum"], 1)

            def s_split(b, r):
                wait(dve, "roped", b, r + 1)
                src = rot[:, r % 2, :].rearrange("p (h d) -> p h d", d=HD)
                dst = ks[:, :, 0] if r == 0 else qs[:, (r - 1) % 2]
                if r >= 3:
                    wait(dve, "qkT_ps", b, r)
                v.tensor_copy(dst[:, :, 0, :], src).then_inc(sg["hi"], 1)
                wait(dve, "hi", b, r + 1)
                v.tensor_tensor(dst[:, :, 1, :], src, dst[:, :, 0, :], ALU.subtract).then_inc(sg["lo"], 1)
                if r == 0:
                    wait(dve, "lo", b, 1)
                    v.tensor_copy(ks[:, :, 1], ks[:, :, 0, ::-1, :]).then_inc(sg["kswap"], 1)

            def s_s(b, g):
                wait(dve, "s_ps", b, g + 1)
                if g >= 2:
                    wait(dve, "expd", b, 4 * (g - 1))
                dve.sem_inc(passed, 1)
                for j in range(GRP):
                    h = GRP * g + j
                    v.tensor_tensor_reduce(out=sm[:, g % 2, j, :], in0=A[g % 2][:, j * P:(j + 1) * P], in1=c("causal"),
                                           scale=1.0, scalar=3.0e38, op0=ALU.add, op1=ALU.min,
                                           accum_out=nmax[:, h:h + 1]).then_inc(sg["masked"], 1)

            def s_p(b, g):
                wait(dve, "expd", b, GRP * (g + 1))
                v.reciprocal(rinv[:, GRP * g:GRP * (g + 1)], ssum[:, GRP * g:GRP * (g + 1)]).then_inc(sg["rsum"], 1)

            def s_o(b, _):
                wait(dve, "o_ps", b, 1)
                wait(dve, "xres", b, 1)
                v.tensor_tensor(x1[:], A[0][:, 0:D], xres[:], ALU.add).then_inc(sg["x1"], 1)

            def r_ln2(b, _):
                layernorm(b, x1, st2, mv2, rs2, xn2, 2, lambda: wait(dve, "x1", b, 1))

            def r_proj(b, n):
                pass

            def r_rope(b, n):
                bank = (Bk[1], Bk[0])[n]
                bias = 2 * (1 - n)
                tab = ("xk_cos", "xk_sin") if n == 0 else ("xq_cos", "xq_sin")
                wait(dve, "xproj", b, (1, 3)[n])
                if n:
                    wait(dve, "xr_sum", b, 1)
                for m, dst in enumerate((xr_a, xr_b)):
                    v.scalar_tensor_tensor(out=dst[:], in0=bank[:, m * T:(m + 1) * T], scalar=colb[:, bias + m:bias + m + 1],
                                           in1=c(tab[m]), op0=ALU.add, op1=ALU.mult).then_inc(sg["xr_mul"], 1)
                wait(dve, "xr_mul", b, 2 * n + 2)
                v.tensor_tensor(xr[:, n, :], xr_a[:], xr_b[:], ALU.add).then_inc(sg["xr_sum"], 1)
                wait(dve, "xr_sum", b, n + 1)
                v.tensor_copy(xhl[:, n, 0, :], xr[:, n, :]).then_inc(sg["xr_hi"], 1)
                wait(dve, "xr_hi", b, n + 1)
                v.tensor_tensor(xhl[:, n, 1, :], xr[:, n, :], xhl[:, n, 0, :], ALU.subtract).then_inc(sg["xr_lo"], 1)
                if n == 0:
                    wait(dve, "xproj", b, 2)
                    v.tensor_tensor(vaug[:, :, :, 0:XC], Bk[2][:, 0:TB * P].rearrange("p (m h c) -> p m h c", m=TB, c=XC),
                                    rowb[:, R_XBV:R_XBV + P].rearrange("p (o h c) -> p o h c", o=1, c=XC).to_broadcast([P, TB, XH, XC]),
                                    ALU.add).then_inc(sg["xv"], 1)

            def r_kz(b, _):
                wait(dve, "kst", b, 2)
                for j in range(XJ):
                    r = slice(32 * j, 32 * j + 32)
                    v.tensor_copy(kz[r, :, j, :], kst[r, :, :]).then_inc(sg["kz"], 1)

            def r_nat(b, h):
                wait(dve, "nat_ps", b, h + 1)
                v.tensor_reduce(xnm[:, h // XJ, h % XJ, :], Bk[h % 2].rearrange("p (m t) -> p m t", m=TB), AX.X,
                                ALU.min).then_inc(sg["xmax"], 1)

            def r_m(b, _):
                wait(dve, "xmax", b, XH)
                for m in range(TB):
                    last = v.tensor_scalar(mt[:, m, :, :].rearrange("p g (j r) -> p g j r", r=32)[:, :, :, MROW], xnm[:, :, :, m],
                                           -1.0 / MSCALE, None, ALU.mult)
                last.then_inc(sg["mt"], 1)
                wait(dve, "mrow", b, 1)
                v.tensor_tensor(qaug[:], qst[:], mrow[:], ALU.add).then_inc(sg["qaug"], 1)

            def r_nrm(b, hg):
                wait(dve, "bc_ps", b, hg + 1)
                if hg >= 2:
                    wait(dve, "onorm", b, hg - 1)
                v.reciprocal(bcs[:, hg % 2, :], Bk[hg % 2][:, T:2 * T]).then_inc(sg["bc"], 1)

            def r_wo(b, _):
                wait(dve, "wo_ps", b, 1)
                v.scalar_tensor_tensor(out=x2[:], in0=Bk[0][:, 0:T], scalar=colb[:, 4:5], in1=x1[:],
                                       op0=ALU.add, op1=ALU.add).then_inc(sg["x2"], 1)

            def r_ln3(b, _):
                layernorm(b, x2, st3, mv3, rs3, xn3, 3, lambda: wait(dve, "x2", b, 1))

            def r_t3(b, _):
                wait(dve, "x3h", b, 1)
                v.tensor_tensor(x3[:, 1], Bk[1][:, 0:D].rearrange("p (k s) -> p k s", k=KD), x3[:, 0], ALU.subtract).then_inc(sg["x3l"], 1)

            def r_ff(b, f):
                u, g = ((Bk[0], Bk[2]), (Bk[3], Bk[1]))[f]
                wait(dve, "ftanh", b, f + 1)
                v.scalar_tensor_tensor(out=fe[:, f, :], in0=fe[:, f, :], scalar=1.0, in1=u, op0=ALU.add, op1=ALU.mult).then_inc(sg["fact"], 1)
                wait(dve, "ff_ps", b, 2 * f + 2)
                wait(dve, "fact", b, f + 1)
                v.scalar_tensor_tensor(out=fe[:, f, :], in0=fe[:, f, :], scalar=HS, in1=g, op0=ALU.mult, op1=ALU.mult).then_inc(sg["fhid"], 1)
                wait(dve, "fh", b, f + 1)
                part = slice(f * (ET // 2), (f + 1) * (ET // 2))
                fh4 = fe[:, f, :].rearrange("p (e s) -> p e s", s=P)
                v.tensor_tensor(hid[:, 1, part, :], fh4, hid[:, 0, part, :], ALU.subtract).then_inc(sg["fl"], 1)

            def r_down(b, _):
                wait(dve, "dn_ps", b, 1)
                dve.wait_ge(out_free, b + 1)
                v.scalar_tensor_tensor(out=outt[:], in0=Bk[0][:, 0:D], scalar=small[:, 16:17], in1=x2[:],
                                       op0=ALU.mult, op1=ALU.add).then_inc(sg["outt"], 1)

            v.memset(mt[:], 0.0).then_inc(zeroed, 1)
            v.memset(kz[:], 0.0).then_inc(zeroed, 1)
            v.memset(vaug[:], 0.0).then_inc(zeroed, 1)
            dve.wait_ge(zeroed, 4)
            v.memset(vaug[:, :, :, XC:2 * XC], 1.0).then_inc(zeroed, 1)
            dve.wait_ge(zeroed, 5)
            dve.wait_ge(d_const, 32)
            dve.wait_ge(d_row, 32)
            kw = rowb[:, R_KW:R_KW + NH].rearrange("p (h o) -> p h o", o=1).to_broadcast([P, NH, HD])
            for dst, name in ((cq, "cos"), (sq, "sin")):
                tab = c(name).rearrange("p (o d) -> p o d", o=1).to_broadcast([P, NH, HD])
                v.scalar_tensor_tensor(out=dst[:], in0=tab, scalar=-float(HD) ** -0.5, in1=kw, op0=ALU.mult, op1=ALU.mult).then_inc(tabs, 1)
            dve.wait_ge(tabs, 2)
            n_rb = 0
            for r in range(5):
                at = R_K if r == 0 else R_Q + 512 * (r - 1)
                for ins in rotate(r, rowb[:, at:at + 512], rot[:, 0, :]):
                    ins.then_inc(rbs, 1)
                    n_rb += 1
                dve.wait_ge(rbs, n_rb)
                v.tensor_tensor(rowb[:, at:at + 512], rot[:, 0, :], rot_b[:], ALU.add).then_inc(rbs, 1)
                n_rb += 1
                dve.wait_ge(rbs, n_rb)
            dve.wait_ge(d_mask, 32)
            v.tensor_scalar(nbn[:].rearrange("p m t -> p (m t)"), maskn, 0.0, None, ALU.is_equal).then_inc(nbs, 1)
            v.tensor_scalar(nbt[:].rearrange("p m t -> p (m t)"), maskt, 0.0, None, ALU.is_equal).then_inc(nbs, 1)
            for m, s in enumerate((HUGE, -HUGE)):
                v.tensor_scalar(bigi[:, m, :], ident, s, None, ALU.mult).then_inc(nbs, 1)
            dve.wait_ge(nbs, 4)
            v.tensor_reduce(small[:, 3:4], nbn[:], AX.XY, ALU.max).then_inc(ffsum, 1)
            dve.wait_ge(nbs, 4)
            dve.wait_ge(totals, 1)
            v.tensor_scalar(small[:, 4:7], Bk[0][:, 0:3], 1.0 / (D * E), EPS_Q, ALU.mult, ALU.add).then_inc(scales, 1)
            v.tensor_copy(flag[:], Bk[0][:, 3:4]).then_inc(flagged, 1)
            dve.wait_ge(scales, 1)
            v.tensor_scalar(small[:, 8:11], small[:, 4:7], 0.5, None, ALU.mult).then_inc(scales, 1)
            v.tensor_scalar(small[:, 12:15], small[:, 4:7], -0.5, None, ALU.mult).then_inc(scales, 1)
            v.tensor_scalar(small[:, 18:19], small[:, 4:5], 0.5, None, ALU.mult).then_inc(scales, 1)
            v.tensor_tensor(small[:, 17:18], small[:, 4:5], small[:, 5:6], ALU.mult).then_inc(scales, 1)
            dve.wait_ge(scales, 5)
            v.scalar_tensor_tensor(out=small[:, 16:17], in0=small[:, 17:18], scalar=0.5 / HS, in1=small[:, 6:7],
                                   op0=ALU.mult, op1=ALU.mult).then_inc(scales, 1)
            for n in range(3):
                v.tensor_scalar(tern[:, n, :], ffw[:, n, :], small[:, 12 + n:13 + n], None, ALU.is_lt).then_inc(scales, 1)
                dve.wait_ge(scales, 7 + n)
                v.scalar_tensor_tensor(out=tern[:, n, :], in0=ffw[:, n, :], scalar=small[:, 8 + n:9 + n], in1=tern[:, n, :],
                                       op0=ALU.is_gt, op1=ALU.subtract).then_inc(terns, 1)
            dve.wait_ge(terns, 3)

            none = lambda b, n: None
            batches(dve, dict(ln=s_ln, qkv=s_qkv, split=s_split, tr=none, s=s_s, p=s_p, o=s_o),
                    dict(ln2=r_ln2, proj=none, rope=r_rope, sel=none, kz=r_kz, nat=r_nat, m=r_m, st=none, pv=none, nrm=r_nrm,
                         wo=r_wo, ln3=r_ln3, t3=r_t3, ff=r_ff, down=r_down))

        @block.scalar
        def _(act):
            a = nc.scalar
            act.dma_start(rowb[:], rows.to_broadcast([P, WROW])).then_inc(d_row, 16)
            act.dma_start(colb[:], cols).then_inc(d_row, 16)
            act.dma_start(k16[:], c16).then_inc(d_const, 16)
            act.dma_start(xw_sb[:], xw).then_inc(d_x, 16)
            act.dma_start(xwo_sb[:], xwo).then_inc(d_x, 16)
            act.dma_start(ffw[:, 1, :], w_gate).then_inc(d_ffw[1], 16)
            act.dma_start(ffw[:, 2, :], w_down).then_inc(d_ffw[2], 16)
            act.dma_start(maskn, mask_n).then_inc(d_mask, 16)
            act.dma_start(maskt, mask_t).then_inc(d_mask, 16)
            act.wait_ge(nbs, 2)
            act.dma_start(ffw[:, 0, :], w_up).then_inc(d_ffw[0], 16)
            for n in (1, 2, 0):
                act.wait_ge(d_ffw[n], 16)
                a.activation(tern[:, n, :], ffw[:, n, :], ACT.Abs, accum_out=small[:, n:n + 1]).then_inc(ffsum, 1)
            act.wait_ge(ffsum, 4)

            def s_ln(b, _):
                wait(act, "xnT_ps", b, 1)
                a.copy(xnT[:].rearrange("p k s -> p (k s)"), A[2][:, 0:D]).then_inc(sg["xnT"], 1)

            def s_tr(b, n):
                wait(act, "qkT_ps", b, n + 1)
                dst = kT[:, 4 * n:4 * n + 4].rearrange("p g v s -> p (g v s)") if n < 2 else \
                    qT[:, 8 * (n - 2):8 * (n - 1)].rearrange("p h s -> p (h s)")
                a.copy(dst, A[2].bitcast(F16)).then_inc(sg["qkT"], 1)

            def s_s(b, g):
                if g >= 2:
                    wait(act, "pT_ps", b, g - 1)
                for j in range(GRP):
                    h = GRP * g + j
                    wait(act, "masked", b, h + 1)
                    a.activation(ex[:, g % 2, j, :], sm[:, g % 2, j, :], ACT.Exp, bias=nmax[:, h:h + 1], scale=-1.0,
                                 accum_out=ssum[:, h:h + 1]).then_inc(sg["expd"], 1)

            def s_p(b, g):
                wait(act, "pT_ps", b, g + 1)
                if g >= 2:
                    wait(act, "pv", b, g - 1)
                a.copy(pT[:, g % 2, :], A[2]).then_inc(sg["pT"], 1)
                if g % 2:
                    wait(act, "pv", b, g + 1)
                    a.copy(oT[:, g // 2].rearrange("p j s -> p (j s)"), A[3]).then_inc(sg["oT"], 1)

            def r_sel(b, n):
                for m in range(2):
                    wait(act, "sel_ps", b, 2 * n + m + 1)
                    bank = (Bk[3], Bk[1], Bk[0], Bk[2])[2 * n + m]
                    dst = (kst, qst)[n][:, 2 * m:2 * m + 2, :].rearrange("p g t -> p (g t)")
                    if n == 0:
                        a.activation(dst, bank, ACT.Identity, bias=c("kcol")).then_inc(sg["kst"], 1)
                    else:
                        a.copy(dst, bank).then_inc(sg["qst"], 1)

            def r_m(b, _):
                wait(act, "mt_ps", b, 1)
                a.copy(mrow[:].rearrange("p g t -> p (g t)"), Bk[2].bitcast(F16)).then_inc(sg["mrow"], 1)

            def r_st(b, h):
                wait(act, "st_ps", b, h + 1)
                if h >= 2:
                    wait(act, "xpv", b, h - 1)
                a.activation(ffw[:, 0, 512 * (h % 2):512 * (h % 2) + 512], Bk[2 + h % 2], ACT.Exp, scale=-1.0).then_inc(sg["xexp"], 1)

            def r_nrm(b, hg):
                wait(act, "xpv", b, XJ * (hg + 1))
                a.copy(oraw[:, hg, :], Bk[hg % 2][:, 0:T]).then_inc(sg["oraw"], 1)

            def r_t3(b, _):
                wait(act, "x3T_ps", b, 1)
                a.copy(x3[:, 0], Bk[1][:, 0:D].rearrange("p (k s) -> p k s", k=KD)).then_inc(sg["x3h"], 1)

            def r_ff(b, f):
                u = (Bk[0], Bk[3])[f]
                wait(act, "ff_ps", b, 2 * f + 1)
                a.activation(fe[:, f, :], u, ACT.Tanh, scale=small[:, 18:19]).then_inc(sg["ftanh"], 1)
                wait(act, "fhid", b, f + 1)
                part = slice(f * (ET // 2), (f + 1) * (ET // 2))
                a.copy(hid[:, 0, part, :], fe[:, f, :].rearrange("p (e s) -> p e s", s=P)).then_inc(sg["fh"], 1)

            none = lambda b, n: None
            act.wait_ge(scales, 4)
            batches(act, dict(ln=s_ln, qkv=none, split=none, tr=s_tr, s=s_s, p=s_p, o=none),
                    dict(ln2=none, proj=none, rope=none, sel=r_sel, kz=none, nat=none, m=r_m, st=r_st, pv=none, nrm=r_nrm,
                         wo=none, ln3=none, t3=r_t3, ff=r_ff, down=none))

        @block.gpsimd
        def _(pool):
            g_ = nc.gpsimd
            pool.wait_ge(pool_set, 1)
            pool.wait_ge(d_row, 32)
            pool.wait_ge(rbs, 15)
            pool.wait_ge(zeroed, 1)

            def s_ln(b, _):
                pool.wait_ge(x_in, b * 16 + 16)
                if type(b) is not int:
                    wait(pool, "x1", b - 1, 1)
                g_.tensor_tensor(xres[:], x_sb[:], rowb[:, R_BO:R_BO + D], ALU.add).then_inc(sg["xres"], 1)
                power(b, mv1, rs1, 1)

            def power(b, mv, rs, n):
                wait(pool, f"ln{n}", b, 3)
                g_.tensor_tensor(rs[:], mv[:, 2:3], half[:], ALU.pow).then_inc(sg[f"rstd{n}"], 1)

            def s_split(b, r):
                wait(pool, "rope_sum", b, r + 1)
                at = R_K if r == 0 else R_Q + 512 * (r - 1)
                g_.tensor_tensor(rot[:, r % 2, :], rot[:, r % 2, :], rowb[:, at:at + 512], ALU.add).then_inc(sg["roped"], 1)

            def s_p(b, g):
                wait(pool, "rsum", b, g + 1)
                r = rinv[:, GRP * g:GRP * (g + 1)].rearrange("p (j o) -> p j o", o=1).to_broadcast([P, GRP, P])
                g_.tensor_tensor(ex[:, g % 2], ex[:, g % 2], r, ALU.mult).then_inc(sg["normed"], 1)

            def r_nrm(b, hg):
                wait(pool, "bc", b, hg + 1)
                g_.tensor_tensor(oraw[:, hg, :], oraw[:, hg, :], bcs[:, hg % 2, :], ALU.mult).then_inc(sg["onorm"], 1)

            none = lambda b, n: None
            batches(pool, dict(ln=s_ln, qkv=none, split=s_split, tr=none, s=none, p=s_p, o=none),
                    dict(ln2=lambda b, _: power(b, mv2, rs2, 2), proj=none, rope=none, sel=none, kz=none, nat=none, m=none, st=none,
                         pv=none, nrm=r_nrm, wo=none, ln3=lambda b, _: power(b, mv3, rs3, 3), t3=none, ff=none, down=none))


def constants():
    f = np.float32
    c32 = np.zeros((P, W32), f)

    def put(name, a):
        c32[:, C32[name][0]:C32[name][1]] = a

    put("ident", np.eye(P, dtype=f))
    s = np.arange(P)
    put("causal", np.where(s[None, :] > s[:, None], f(BIG), f(0)))
    inv = (f(1) / f(10000.0) ** (np.arange(0, HD, 2, dtype=f) / f(HD))).astype(f)
    ang = np.arange(S, dtype=f)[:, None] * inv[None, :]
    put("cos", np.concatenate([np.cos(ang), np.cos(ang)], 1))
    put("sin", np.concatenate([-np.sin(ang), np.sin(ang)], 1))
    rd = XC // 2
    th = (f(1) / f(10000.0) ** (np.arange(0, rd, 2, dtype=f) / f(rd))).astype(f)
    ang = (np.arange(T, dtype=f)[:, None] * th[None, :]).T
    cosx, sinx = np.ones((XC, T), f), np.zeros((XC, T), f)
    cosx[0:2], cosx[2:4] = np.cos(ang), np.cos(ang)
    sinx[0:2], sinx[2:4] = -np.sin(ang), np.sin(ang)
    cosx, sinx = np.tile(cosx, (XH, 1)), np.tile(sinx, (XH, 1))
    put("xk_cos", cosx)
    put("xk_sin", sinx)
    scale = f(-1.0 / np.sqrt(XC))
    put("xq_cos", cosx * scale)
    put("xq_sin", sinx * scale)
    row = np.arange(P)
    put("kcol", np.where(row % 32 == MROW, f(MSCALE), f(0))[:, None])
    put("selsum", np.where(row[:, None] == 32 * (row[None, :] // 32) + XC, f(1), f(0)))
    c16 = np.zeros((P, W16), np.float16)
    c16[:, 0:P] = np.eye(P)
    c16[:, P:2 * P] = 10000.0 * np.eye(P)
    for name, slots in (("k_hi", (0, 2)), ("k_lo", (1,)), ("q_hi", (0, 1)), ("q_lo", (2,))):
        for hg in range(XG):
            for j in range(XJ):
                for r in slots:
                    for d in range(XC):
                        c16[(hg * XJ + j) * XC + d, C16[name][0] + hg * P + 32 * j + XC * r + d] = 1.0
    return c32, c16


def kernel(**inputs):
    import concourse.bacc as bacc
    from concourse.bass_utils import run_bass_kernel_spmd

    a = {k: np.asarray(v) for k, v in inputs.items()}

    def tiles(w):
        k, n = w.shape
        return w.reshape(k // P, P, n).transpose(1, 0, 2)

    wq, wk, wv = a["L0_attn_Wq"].T, a["L0_attn_Wk"].T, a["L0_attn_Wv"].T
    perm = np.arange(P).reshape(XH, XC)[:, [2, 3, 0, 1, 4, 5, 6, 7]].ravel()
    xwq, xwk, xwv = a["L0_xattn_wq"], a["L0_xattn_wk"], a["L0_xattn_wv"]
    xbq, xbk = a["L0_xattn_bq"], a["L0_xattn_bk"]
    xwo = np.zeros((XJ, 32, XG, P), np.float32)
    xwo[:, 0:XC] = a["L0_xattn_wo"].T.reshape(XG, XJ, XC, P).transpose(1, 2, 0, 3)
    mask = a["mask_1x1x2048x2048_if1"].reshape(T, T)
    c32, c16 = constants()
    arrays = dict(
        x=a["x"], ctx=a["ctx_2048"],
        mask_n=mask.reshape(TB, P, T).transpose(1, 0, 2).reshape(P, TB * T),
        mask_t=mask.T.reshape(TB, P, T).transpose(1, 0, 2).reshape(P, TB * T),
        w_qkv=tiles(np.concatenate([wk, wv, wq], 1)),
        w_o=a["L0_attn_Wo"].T.reshape(NPAIR, 2, GRP, HD, D).transpose(1, 3, 0, 2, 4).reshape(P, NPAIR, GRP, D),
        rows=np.concatenate([a["L0_attn_bk"], a["L0_attn_bv"], a["L0_attn_bq"], a["L0_attn_bo"], a["L0_xattn_bv"],
                             a["L0_attn_key_weights"]])[None],
        cols=np.stack([xbq, xbq[perm], xbk, xbk[perm], a["L0_xattn_bo"]], 1),
        xw=np.stack([xwq.T, xwq[perm].T, xwk.T, xwk[perm].T, xwv.T], 1),
        xwo=xwo.reshape(P, XG, P),
        w_up=tiles(a["L0_ffn_W_up"].T).reshape(P, KD * E),
        w_gate=tiles(a["L0_ffn_W_gate"].T).reshape(P, KD * E),
        w_down=tiles(a["L0_ffn_W_down"].T).reshape(P, ET * D),
        c32=c32, c16=c16)
    arrays = {k: np.ascontiguousarray(v) for k, v in arrays.items()}
    nc = bacc.Bacc("TRN2", target_bir_lowering=False, num_devices=1)
    aps = {k: nc.dram_tensor(f"in_{k}", v.shape, mybir.dt.from_np(v.dtype), kind="ExternalInput").ap() for k, v in arrays.items()}
    out = nc.dram_tensor("out_0", (B, S, D), F32, kind="ExternalOutput").ap()
    build(nc, *aps.values(), out)
    r = run_bass_kernel_spmd(nc, [{f"in_{k}": v for k, v in arrays.items()}], core_ids=[0])
    return r.results[0]["out_0"]
```

```python
from contextlib import ExitStack

import numpy as np
import concourse.bass as bass
from concourse import mybir

F32 = mybir.dt.float32
F16 = mybir.dt.float16
BF16 = mybir.dt.bfloat16
I32 = mybir.dt.int32
ALU = mybir.AluOpType
ACT = mybir.ActivationFunctionType
AX = mybir.AxisListType

B, S, D = 8, 128, 256
P = 128
KD = D // P
NH, NKV, HD = 32, 8, 64
GRP = NH // NKV
NPAIR = NKV // 2
XH, XC, XG = 16, 8, 4
XJ = XH // XG
T = D
TB = T // P
E = 1024
ET = E // P
NF = ET // 2
BIG = 1.0e30
MROW, MSCALE = 24, 256.0
HS = 1.0 / 32
EPS_LN, EPS_Q = 1e-5, 1e-8
HUGE = 2.0 ** 100

C32 = {}
_at = 0
for _n, _w in (("ident", P), ("causal", P), ("cos", HD), ("sin", HD), ("xk_cos", T), ("xk_sin", T),
               ("xq_cos", T), ("xq_sin", T), ("kcol", 1), ("selsum", P)):
    C32[_n] = (_at, _at + _w)
    _at += _w
W32 = _at
C16 = {"ident": (0, P), "ten": (P, 2 * P), "k_hi": (256, 768), "k_lo": (768, 1280), "q_hi": (1280, 1792), "q_lo": (1792, 2304)}
W16 = 2304
NQKV = (NH + 2 * NKV) * HD
R_K, R_V, R_Q = 0, NKV * HD, 2 * NKV * HD
R_BO, R_XBV, R_KW = NQKV, NQKV + D, NQKV + D + P
WROW = NQKV + D + P + NH

SELF_SIGNALS = dict(
    ln1=3, rstd1=1, xn1=1, xres=1, xnT_ps=1, xnT=1,
    qkv_ps=6, rope_mul=10, biased=5, roped=5, hi=5, lo=5, kswap=1, v_sb=1,
    qkT_ps=6, qkT=6, s_ps=8, masked=32, expd=32, rsum=8, normed=8, pT_ps=8, pT=8, pv=8, oT=4, o_ps=1, x1=1)
CROSS_SIGNALS = dict(
    ln2=3, rstd2=1, xn2=1, xproj=3, xr_mul=4, xr_sum=2, xr_hi=2, xr_lo=2, xv=1, sel_ps=4, kst=2, qst=2, kz=4,
    nat_ps=16, xmax=16, mt=1, mt_ps=1, mrow=1, qaug=1, st_ps=16, xexp=16, xpv=16, oraw=4, bc_ps=4, bc=4, onorm=4,
    wo_ps=1, x1r=1, x2=1)
FFN_SIGNALS = dict(
    ln3=3, rstd3=1, xn3=1, x3T_ps=1, x3h=1, x3l=1,
    ff_ps=NF, ftanh=NF, fact=NF, fhid=NF, fh=NF, fl=NF, dn_ps=1, outt=1)


ORDER = """
S.ln_stats C.transposed0 C.transposed1 C.transposed2 S.ln_apply C.pv0 C.pv1 C.transposed3 C.pv2 C.exp0 C.exp1 C.exp2
S.transpose_x C.transposed4 S.qkv0 S.bias0 S.qkv1 C.exp3 S.rope0 S.v_out C.pv3 S.qkv2 C.exp4 C.transposed5
C.transposed6 S.rope1 S.bias1 C.out0 S.high0 C.pv4 C.exp5 C.sums0 S.bias2 S.qkv3 C.exp6 C.pv5 S.low0 C.exp7 S.rope2
C.exp8 C.scale0 C.transposed7 C.transposed8 C.pv6 S.transpose0 S.qkv4 S.bias3 C.recip0 S.low1 C.pv7 S.high1
S.transpose1 S.rope3 S.qkv5 S.low2 S.high2 S.rope4 S.bias4 C.transposed9 C.out1 C.transposed10 C.exp9 S.transpose2
C.pv8 C.sums1 S.scores0 C.exp10 C.pv9 S.high3 C.transposed11 K.ln_stats C.exp11 S.transpose3 C.scale1 C.exp12 C.recip1
C.exp13 S.mask0 S.low3 S.high4 S.low4 C.transposed12 C.pv10 C.out2 C.transposed13 C.exp14 C.exp15 C.out3 C.pv11
S.scores1 C.recip2 C.transposed14 C.pv12 C.pv13 C.transposed15 S.transpose4 C.sums2 C.pv14 C.pv15 S.exp0 S.scores2
C.sums3 C.recip3 C.wo C.scale2 C.scale3 S.mask1 S.transpose5 S.exp1 S.copy_p0 K.ln_apply C.x2_out F.ln_stats K.proj_k
S.recip0 K.rope_k F.ln_apply K.proj_v S.transpose_p0 K.v_out K.spread0 S.recip1 F.transpose_x S.scores3 S.mask2
S.mask3 S.pv0 K.proj_q S.exp2 S.copy_p1 F.low_x K.rope_q S.transpose_p1 S.exp3 S.recip2 S.mask4 S.recip3 S.scores4
S.scores5 F.act0 F.up_gate0 F.tanh0 K.spread1 K.spread2 S.o_out0 S.pv1 K.spread3 S.copy_p2 F.tanh1 S.transpose_p2
K.zero_k S.exp4 S.mask5 F.up_gate1 F.up_gate2 S.scores6 S.transpose_p3 F.high0 S.pv2 S.recip4 S.copy_p3 F.act1
K.scores0 K.max0 F.tanh2 S.exp5 K.scores1 F.tanh3 S.pv3 S.o_out1 S.mask6 S.copy_p4 S.exp6 K.keep F.up_gate3 F.high1
F.high2 K.scores2 F.low0 S.recip5 S.copy_p5 K.max1 F.act2 S.transpose_p4 S.scores7 S.wo0 F.act3 K.max2 S.transpose_p5
S.pv4 S.recip6 K.scores3 F.low1 K.scores4 F.high3 F.low2 F.low3 S.exp7 S.o_out2 S.mask7 S.pv5 F.down K.scores5
S.transpose_p6 S.copy_p6 K.max3 K.scores6 K.scores7 K.max4 K.scores8 K.scores9 S.wo1 K.scores10 K.scores11 K.scores12
F.out K.scores13 K.max5 S.recip7 K.max6 S.wo2 K.max7 K.max8 S.copy_p7 S.o_out3 K.max9 K.scores14 S.transpose_p7
K.max10 K.scores15 S.pv6 K.max11 S.pv7 K.max12 K.max13 K.max14 K.max_transpose S.wo3 K.max15 K.max_pack K.add_max
S.x1_out
"""


def parsed(word):
    chain, step = word.split(".")
    name = step.rstrip("0123456789")
    return chain, name, int(step[len(name):] or 0)


BODY = [parsed(word) for word in ORDER.split()]


def steps_of(chains):
    return [step for step in BODY if step[0] in chains]


def first_steps():
    o = []
    for step in steps_of("S"):
        o.append(step)
        for after, n in (((("S", "scores", 0)), 0), (("S", "scores", 2), 1), (("S", "scores", 3), 2), (("S", "scores", 4), 3), (("S", "scores", 5), 4)):
            if step == after:
                o.append(("W", "weights", n))
    return o


def build(nc, x, ctx, mask_n, mask_t, w_qkv, w_o, rows, cols, xw, xwo, w_up, w_gate, w_down, c32, c16, out):
    with ExitStack() as st:
        def sb(name, shape, dt=F32):
            return st.enter_context(nc.sbuf_tensor(name, shape, dt))

        def sem(name):
            return st.enter_context(nc.semaphore(name))

        k32 = sb("k32", [P, W32])
        k16 = sb("k16", [P, W16], F16)
        rowb = sb("rowb", [P, WROW])
        colb = sb("colb", [P, 5])
        wqkv = sb("wqkv", [P, KD, NQKV])
        wo = sb("wo", [P, NPAIR, GRP, D])
        xw_sb = sb("xw_sb", [P, 5, P])
        xwo_sb = sb("xwo_sb", [P, XG, P])
        ffw = sb("ffw", [P, 3, KD * E])
        tern = sb("tern", [P, 3, KD * E], F16)
        cq = sb("cq", [P, NH, HD])
        sq = sb("sq", [P, NH, HD])
        maskn = ffw[:, 0, 0:512].bitcast(I32)
        maskt = ffw[:, 0, 512:1024].bitcast(I32)
        nbn = sb("nbn", [P, TB, T], F16)
        nbt = sb("nbt", [P, TB, T], F16)
        bigi = sb("bigi", [P, 2, P], BF16)
        small = sb("small", [P, 32])
        flag = sb("flag", [P, 1], I32)
        half = sb("half", [P, 1])
        ones = sb("ones", [P, P])
        ident = k32[:, C32["ident"][0]:C32["ident"][1]]
        ident16 = k16[:, 0:P]

        def c(name):
            return k32[:, C32[name][0]:C32[name][1]]

        x_sb = sb("x_sb", [P, D])
        xres = sb("xres", [P, D])
        xn1 = sb("xn1", [P, D])
        xnT = sb("xnT", [P, KD, P])
        st1, mv1, rs1 = sb("st1", [P, 6]), sb("mv1", [P, 3]), sb("rs1", [P, 1])
        rot_b = sb("rot_b", [P, 2, 512])
        rot = sb("rot", [P, 2, 512])
        qs = sb("qs", [P, 2, 8, 2, HD], F16)
        ks = sb("ks", [P, NKV, 2, 2, HD], F16)
        v_sb = sb("v_sb", [P, NKV * HD])
        qT = sb("qT", [P, NH, P], F16)
        kT = sb("kT", [P, NKV, 2, P], F16)
        sm = sb("sm", [P, 2, GRP, P])
        ex = sb("ex", [P, 2, GRP, P])
        nmax = sb("nmax", [P, NH])
        ssum = sb("ssum", [P, NH])
        rinv = sb("rinv", [P, NH])
        pT = sb("pT", [P, 2, GRP * P])
        oT = sb("oT", [P, NPAIR, GRP, P])
        x1 = sb("x1", [P, D])
        ctx_sb = sb("ctx_sb", [P, D])
        xn2 = sb("xn2", [P, T])
        st2, mv2, rs2 = sb("st2", [P, 6]), sb("mv2", [P, 3]), sb("rs2", [P, 1])
        xr_a = sb("xr_a", [P, T])
        xr_b = sb("xr_b", [P, T])
        xr = sb("xr", [P, 2, T])
        xhl = sb("xhl", [P, 2, 2, T], F16)
        kst = sb("kst", [P, XG, T], F16)
        qst = sb("qst", [P, XG, T], F16)
        mrow = kst
        qaug = sb("qaug", [P, XG, T], F16)
        kz = sb("kz", [P, XG, XJ, T], F16)
        vaug = sb("vaug", [P, TB, XH, 32])
        xnm = sb("xnm", [P, XG, XJ, TB])
        mt = sb("mt", [P, TB, XG, P], F16)
        xpT = ffw[:, 0, 0:1024].rearrange("p (n m t) -> p n m t", n=2, m=TB)
        oraw = ffw[:, 0, 1024:2048].rearrange("p (g t) -> p g t", g=XG)
        bcs = ffw[:, 2, 0:512].rearrange("p (n t) -> p n t", n=2)
        x2 = ffw[:, 2, 512:768]
        x1r = ffw[:, 2, 1536:1792]
        xn3 = ffw[:, 2, 768:1024]
        st3, mv3, rs3 = sb("st3", [P, 6]), sb("mv3", [P, 3]), sb("rs3", [P, 1])
        x3 = ffw[:, 2, 1024:1280].bitcast(F16).rearrange("p (v k s) -> p v k s", v=2, k=KD)
        hid = ffw[:, 1, 1024:2048].bitcast(F16).rearrange("p (v e s) -> p v e s", v=2, e=ET)
        outt = ffw[:, 2, 1280:1536]

        PS = st.enter_context(nc.psum_tensor("PS", [P, 8, 512], F32))
        A = [PS[:, n, :] for n in range(4)]
        Bk = [PS[:, n, :] for n in range(4, 8)]
        def scores_bank(h):
            return Bk[h % 2 if h < 6 else (h - 4) % 4]

        QB = (A[0], A[1], A[3])
        fe = ffw[:, 1, 0:1024].rearrange("p (f n) -> p f n", f=NF)

        sg = {n: sem(n) for n in (*SELF_SIGNALS, *CROSS_SIGNALS, *FFN_SIGNALS)}
        per = {**SELF_SIGNALS, **CROSS_SIGNALS, **FFN_SIGNALS}
        x_in, ctx_in, out_st, out_free = sem("x_in"), sem("ctx_in"), sem("out_st"), sem("out_free")
        d_const, d_row, d_wkv, d_wq, d_wo, d_x, d_mask = (sem(n) for n in ("d_const", "d_row", "d_wkv", "d_wq", "d_wo", "d_xw", "d_mask"))
        d_ffw = [sem(f"d_ffw{n}") for n in range(3)]
        tabs, rbs, zeroed, nbs, ffsum, totals, scales, terns, pool_set, flagged = (
            sem(n) for n in ("tabs", "rbs", "zeroed", "nbs", "ffsum", "totals", "scales", "terns", "pool_set", "flagged"))
        passed = sem("passed")

        def wait(eng, name, b, k):
            v = b * per[name] + k
            if not (type(v) is int and v <= 0):
                eng.wait_ge(sg[name], v)

        block = st.enter_context(nc.Block())

        def run(steps, order, **batch):
            for chain, name, n in order:
                if name in steps[chain]:
                    steps[chain][name](batch[chain], n)

        def rounds(eng, steps):
            run(steps, steps_of("SK"), S=1, K=0)
            with eng.Fori(2, B) as i:
                run(steps, BODY, S=i, K=i - 1, C=i - 2, F=i - 2)
            run(steps, steps_of("KCF"), K=B - 1, C=B - 2, F=B - 2)
            run(steps, steps_of("CF"), C=B - 1, F=B - 1)

        @block.sync
        def _(sp):
            sp.sem_inc(out_free, 1)
            sp.dma_start(x_sb[:], x[0]).then_inc(x_in, 16)
            sp.dma_start(k32[:], c32).then_inc(d_const, 16)
            sp.dma_start(wqkv[:, :, 0:2 * NKV * HD], w_qkv[:, :, 0:2 * NKV * HD]).then_inc(d_wkv, 16)
            sp.dma_start(wqkv[:, :, 2 * NKV * HD:], w_qkv[:, :, 2 * NKV * HD:]).then_inc(d_wq, 16)
            sp.dma_start(wo[:], w_o).then_inc(d_wo, 16)
            sp.dma_start(ctx_sb[:], ctx[0]).then_inc(ctx_in, 16)
            sp.wait_ge(sg["xn1"], 1)
            sp.wait_ge(sg["xres"], 1)
            sp.dma_start(x_sb[:], x[1]).then_inc(x_in, 16)

            def load_x(b):
                sp.wait_ge(sg["xn1"], b)
                sp.wait_ge(sg["xres"], b)
                src = x[b] if type(b) is int else x[bass.ds(b, 1)].rearrange("a p n -> (a p) n")
                sp.dma_start(x_sb[:], src).then_inc(x_in, 16)

            def load_ctx(b):
                sp.wait_ge(sg["xproj"], (b - 1) * 3 + 2)
                src = ctx[b] if type(b) is int else ctx[bass.ds(b, 1)].rearrange("a p n -> (a p) n")
                sp.dma_start(ctx_sb[:], src).then_inc(ctx_in, 16)

            def store(b):
                sp.wait_ge(sg["outt"], b + 1)
                dst = out[b] if type(b) is int else out[bass.ds(b, 1)].rearrange("a p n -> (a p) n")
                sp.dma_start(dst, outt[:]).then_inc(out_st, 16)
                sp.wait_ge(out_st, b * 16 + 16)
                sp.sem_inc(out_free, 1)

            load_x(2)
            load_ctx(1)
            with sp.Fori(2, B - 1) as i:
                load_x(i + 1)
                load_ctx(i)
                store(i - 2)
            load_ctx(B - 1)
            for b in range(B - 3, B):
                store(b)

        @block.tensor
        def _(pe):
            mm = nc.tensor.matmul

            def weights(_, n):
                if n == 2:
                    pe.wait_ge(zeroed, 1)
                    pe.wait_ge(ffsum, 4)
                    mm(Bk[0][:, 0:4], ones[:], small[:, 0:4], start=True, stop=True).then_inc(totals, 1)

            def s_transpose_x(b, _):
                wait(pe, "xn1", b, 1)
                if type(b) is not int:
                    wait(pe, "pT", b, 0)
                for k in range(KD):
                    last = nc.tensor.transpose(A[2][:, k * P:(k + 1) * P], xn1[:, k * P:(k + 1) * P], ident)
                last.then_inc(sg["xnT_ps"], 1)

            def s_qkv(b, n):
                if n == 0:
                    wait(pe, "xnT", b, 1)
                    wait(pe, "masked", b, 0)
                    wait(pe, "x1", b, 0)
                    pe.wait_ge(d_wkv, 16)
                elif n == 2:
                    wait(pe, "oT", b, 0)
                    pe.wait_ge(d_wq, 16)
                elif n == 3:
                    wait(pe, "rope_mul", b, 2)
                elif n == 4:
                    wait(pe, "v_sb", b, 1)
                elif n == 5:
                    wait(pe, "rope_mul", b, 4)
                for k in range(KD):
                    last = mm(QB[n % 3], xnT[:, k, :], wqkv[:, k, n * 512:(n + 1) * 512], start=(k == 0), stop=(k == KD - 1))
                last.then_inc(sg["qkv_ps"], 1)

            def s_transpose(b, n):
                if n < 2:
                    wait(pe, "kswap", b, 1)
                    src = [ks[:, g, v] for g in range(4 * n, 4 * n + 4) for v in range(2)]
                else:
                    wait(pe, "lo", b, n)
                    src = [qs[:, n % 2, h] for h in range(8)]
                wait(pe, "qkT", b, n) if n else wait(pe, "xnT", b, 1)
                dst = A[2].bitcast(F16)
                for m, a in enumerate(src):
                    last = nc.tensor.transpose(dst[:, m * P:(m + 1) * P], a.rearrange("p t d -> p (t d)"), ident16)
                last.then_inc(sg["qkT_ps"], 1)

            def s_scores(b, g):
                wait(pe, "qkT", b, 3 + g // 2)
                if g >= 2:
                    wait(pe, "masked", b, 4 * (g - 1))
                else:
                    wait(pe, "rope_mul", b, 6 + 2 * g)
                for j in range(GRP):
                    for v in range(2):
                        last = mm(A[g % 2][:, j * P:(j + 1) * P], qT[:, GRP * g + j, :], kT[:, g, v, :],
                                  start=(v == 0), stop=(v == 1))
                last.then_inc(sg["s_ps"], 1)

            def s_transpose_p(b, g):
                wait(pe, "normed", b, g + 1)
                wait(pe, "pT", b, g) if g else wait(pe, "qkT", b, 6)
                for j in range(GRP):
                    last = nc.tensor.transpose(A[2][:, j * P:(j + 1) * P], ex[:, g % 2, j, :], ident)
                last.then_inc(sg["pT_ps"], 1)

            def s_pv(b, g):
                if g == 0:
                    wait(pe, "v_sb", b, 1)
                    wait(pe, "rope_mul", b, 10)
                if g % 2 == 0 and g:
                    wait(pe, "oT", b, g // 2)
                wait(pe, "pT", b, g + 1)
                e = g % 2
                mm(A[3][HD * e:HD * e + HD, :], v_sb[:, g * HD:(g + 1) * HD], pT[:, g % 2, :],
                   start=True, stop=True).then_inc(sg["pv"], 1)

            def s_wo(b, n):
                if n == 0:
                    pe.wait_ge(d_wo, 16)
                    wait(pe, "masked", b, NH - GRP)
                wait(pe, "oT", b, n + 1)
                for j in range(GRP):
                    last = mm(A[0][:, 0:D], oT[:, n, j, :], wo[:, n, j, :], start=(n == 0 and j == 0), stop=(n == NPAIR - 1 and j == GRP - 1))
                if n == NPAIR - 1:
                    last.then_inc(sg["o_ps"], 1)

            def k_proj_k(b, _):
                pe.wait_ge(d_x, 32)
                pe.wait_ge(ctx_in, b * 16 + 16)
                wait(pe, "x2", b, 0)
                for m in range(2):
                    last = mm(Bk[0][:, m * T:(m + 1) * T], xw_sb[:, 2 + m, :], ctx_sb[:], start=True, stop=True)
                last.then_inc(sg["xproj"], 1)

            def k_proj_v(b, _):
                for m in range(TB):
                    last = mm(Bk[1][:, m * P:(m + 1) * P], ctx_sb[:, m * P:(m + 1) * P], xw_sb[:, 4, :], start=True, stop=True)
                last.then_inc(sg["xproj"], 1)

            def k_proj_q(b, _):
                wait(pe, "xn2", b, 1)
                wait(pe, "xv", b, 1)
                for m in range(2):
                    last = mm(Bk[1][:, m * T:(m + 1) * T], xw_sb[:, m, :], xn2[:], start=True, stop=True)
                last.then_inc(sg["xproj"], 1)

            def k_spread(b, n):
                wait(pe, "xr_lo", b, n // 2 + 1)
                if n == 1:
                    wait(pe, "xr_mul", b, 4)
                elif n >= 2:
                    wait(pe, "kst", b, n - 1)
                for q in range(2):
                    hg = 2 * (n % 2) + q
                    for v, name in enumerate((("k_hi", "k_lo"), ("q_hi", "q_lo"))[n // 2]):
                        at = C16[name][0] + hg * P
                        last = mm(Bk[n % 2][:, q * T:(q + 1) * T], k16[:, at:at + P], xhl[:, n // 2, v, :], start=(v == 0), stop=(v == 1))
                last.then_inc(sg["sel_ps"], 1)

            hidden = {}

            def masked(dst, pairs, stop):
                mm(dst, bigi[:, 0, :], pairs, start=False, stop=False)
                mm(dst, bigi[:, 1, :], pairs, start=False, stop=False)
                return mm(dst, k16[:, P:2 * P], pairs, start=False, stop=stop)

            def k_scores(b, h):
                if h == 0:
                    wait(pe, "kz", b, XJ)
                    wait(pe, "qst", b, 2)
                elif 2 <= h < 6:
                    wait(pe, "xmax", b, h - 1)
                elif h >= 8:
                    wait(pe, "xmax", b, h - 3)
                elif h == 6:
                    wait(pe, "outt", b, 0)

                def products(hide):
                    for m in range(TB):
                        dst = scores_bank(h)[:, m * T:(m + 1) * T]
                        last = mm(dst, qst[:, h // XJ, m * P:(m + 1) * P], kz[:, h // XJ, h % XJ, :], start=True, stop=not hide)
                        if hide:
                            last = masked(dst, nbn[:, m, :], True)
                    last.then_inc(sg["nat_ps"], 1)

                with pe.If(hidden["any"]):
                    products(True)
                with pe.Else():
                    products(False)

            def k_max_transpose(b, _):
                wait(pe, "mt", b, 1)
                dst = Bk[2].bitcast(F16)
                for hg in range(XG):
                    for m in range(TB):
                        last = nc.tensor.transpose(dst[:, hg * T + m * P:hg * T + (m + 1) * P], mt[:, m, hg, :], ident16)
                last.then_inc(sg["mt_ps"], 1)

            def c_transposed(b, h):
                if h == 0:
                    wait(pe, "qaug", b, 1)
                elif h >= 2:
                    wait(pe, "xexp", b, h - 1)

                def products(hide):
                    for m in range(TB):
                        dst = Bk[2 + h % 2][:, m * T:(m + 1) * T]
                        k = kz[:, h // XJ, h % XJ, m * P:(m + 1) * P]
                        if hide:
                            mm(dst, k, qst[:, h // XJ, :], start=True, stop=False)
                            masked(dst, nbt[:, m, :], False)
                            last = mm(dst, k, mrow[:, h // XJ, :], start=False, stop=True)
                        else:
                            last = mm(dst, k, qaug[:, h // XJ, :], start=True, stop=True)
                    last.then_inc(sg["st_ps"], 1)

                with pe.If(hidden["any"]):
                    products(True)
                with pe.Else():
                    products(False)

            def c_pv(b, h):
                hg, j = h // XJ, h % XJ
                wait(pe, "xexp", b, h + 1)
                if j == 0 and hg >= 2:
                    wait(pe, "bc", b, hg - 1)
                for m in range(TB):
                    last = mm(Bk[hg % 2][32 * j:32 * j + 32, 0:T], vaug[:, m, h, :], xpT[:, h % 2, m, :],
                              start=(m == 0), stop=(m == TB - 1))
                last.then_inc(sg["xpv"], 1)

            def c_sums(b, hg):
                wait(pe, "oraw", b, hg + 1)
                mm(Bk[hg % 2][:, T:2 * T], c("selsum"), oraw[:, hg, :], start=True, stop=True).then_inc(sg["bc_ps"], 1)

            def c_wo(b, _):
                wait(pe, "onorm", b, XG)
                for hg in range(XG):
                    last = mm(Bk[0][:, 0:T], xwo_sb[:, hg, :], oraw[:, hg, :], start=(hg == 0), stop=(hg == XG - 1))
                last.then_inc(sg["wo_ps"], 1)

            def f_transpose_x(b, _):
                wait(pe, "xn3", b, 1)
                for k in range(KD):
                    last = nc.tensor.transpose(Bk[3][:, k * P:(k + 1) * P], xn3[:, k * P:(k + 1) * P], ident)
                last.then_inc(sg["x3T_ps"], 1)

            def f_up_gate(b, n):
                if n == 0:
                    wait(pe, "x3l", b, 1)
                elif n >= 2:
                    wait(pe, "fhid", b, n - 1)
                for w in range(2):
                    for e in range(2):
                        at = (2 * n + e) * P
                        for m in range(2 * KD):
                            k, v = m // 2, m % 2
                            last = mm(Bk[2 + n % 2][:, (2 * w + e) * P:(2 * w + e + 1) * P], tern[:, w, k * E + at:k * E + at + P],
                                      x3[:, v, k, :], start=(m == 0), stop=(m == 2 * KD - 1))
                last.then_inc(sg["ff_ps"], 1)

            def f_down(b, _):
                wait(pe, "fl", b, NF)
                for e in range(ET):
                    for v in range(2):
                        last = mm(Bk[2][:, 0:D], hid[:, v, e, :], tern[:, 2, e * D:(e + 1) * D],
                                  start=(e == 0 and v == 0), stop=(e == ET - 1 and v == 1))
                last.then_inc(sg["dn_ps"], 1)

            steps = dict(
                S=dict(transpose_x=s_transpose_x, qkv=s_qkv, transpose=s_transpose, scores=s_scores, transpose_p=s_transpose_p,
                       pv=s_pv, wo=s_wo),
                K=dict(proj_k=k_proj_k, proj_v=k_proj_v, proj_q=k_proj_q, spread=k_spread, scores=k_scores,
                       max_transpose=k_max_transpose),
                C=dict(transposed=c_transposed, pv=c_pv, sums=c_sums, wo=c_wo),
                F=dict(transpose_x=f_transpose_x, up_gate=f_up_gate, down=f_down),
                W=dict(weights=weights))
            pe.wait_ge(d_const, 32)
            run(steps, first_steps(), S=0, W=0)
            pe.wait_ge(flagged, 1)
            pe.wait_ge(terns, 3)
            hidden["any"] = pe.value_load(flag[0:1, 0:1])
            rounds(pe, steps)

        @block.vector
        def _(dve):
            v = nc.vector

            def ln_stats(b, src, stt, mv, n):
                ln = f"ln{n}"
                v.bn_stats(stt[:], src[:]).then_inc(sg[ln], 1)
                wait(dve, ln, b, 1)
                dve.sem_inc(passed, 1)
                v.bn_aggr(mv[:, 0:2], stt[:]).then_inc(sg[ln], 1)
                wait(dve, ln, b, 2)
                v.tensor_scalar(mv[:, 2:3], mv[:, 1:2], EPS_LN, None, ALU.add).then_inc(sg[ln], 1)

            def ln_apply(b, src, mv, rs, dst, n):
                wait(dve, f"rstd{n}", b, 1)
                v.tensor_scalar(dst[:], src[:], mv[:, 0:1], rs[:], ALU.subtract, ALU.mult).then_inc(sg[f"xn{n}"], 1)

            def s_ln_stats(b, _):
                dve.wait_ge(x_in, b * 16 + 16)
                ln_stats(b, x_sb, st1, mv1, 1)

            def tables(r):
                if r == 0:
                    return (c("cos").rearrange("p (o d) -> p o d", o=1).to_broadcast([P, 8, HD]),
                            c("sin").rearrange("p (o d) -> p o d", o=1).to_broadcast([P, 8, HD]))
                return cq[:, 8 * (r - 1):8 * r, :], sq[:, 8 * (r - 1):8 * r, :]

            def rotate(r, src, dst, dst_b):
                cos, sin = tables(r)
                yield v.tensor_tensor(dst.rearrange("p (h d) -> p h d", d=HD), src.rearrange("p (h d) -> p h d", d=HD), cos, ALU.mult)
                yield v.tensor_tensor(dst_b.rearrange("p (h t d) -> p h t d", t=2, d=HD // 2),
                                      src.rearrange("p (h t d) -> p h t d", t=2, d=HD // 2)[:, :, ::-1, :],
                                      sin.rearrange("p h (t d) -> p h t d", t=2), ALU.mult)

            def s_v_out(b, _):
                wait(dve, "qkv_ps", b, 2)
                v.tensor_tensor(v_sb[:], QB[1], rowb[:, R_V:R_V + 512], ALU.add).then_inc(sg["v_sb"], 1)

            def s_rope(b, r):
                n = r + 1 if r else 0
                wait(dve, "qkv_ps", b, n + 1)
                if r >= 2:
                    wait(dve, "lo", b, r - 1)
                for ins in rotate(r, QB[n % 3], rot[:, r % 2, :], rot_b[:, r % 2, :]):
                    ins.then_inc(sg["rope_mul"], 1)

            def s_low(b, r):
                wait(dve, "hi", b, r + 1)
                dst = ks[:, :, 0] if r == 0 else qs[:, (r - 1) % 2]
                v.tensor_tensor(dst[:, :, 1, :], rot[:, r % 2, :].rearrange("p (h d) -> p h d", d=HD), dst[:, :, 0, :],
                                ALU.subtract).then_inc(sg["lo"], 1)
                if r == 0:
                    wait(dve, "lo", b, 1)
                    v.tensor_copy(ks[:, :, 1], ks[:, :, 0, ::-1, :]).then_inc(sg["kswap"], 1)

            def s_mask(b, g):
                wait(dve, "s_ps", b, g + 1)
                if g >= 2:
                    wait(dve, "expd", b, 4 * (g - 1))
                dve.sem_inc(passed, 1)
                for j in range(GRP):
                    h = GRP * g + j
                    v.tensor_tensor_reduce(out=sm[:, g % 2, j, :], in0=A[g % 2][:, j * P:(j + 1) * P], in1=c("causal"),
                                           scale=1.0, scalar=3.0e38, op0=ALU.add, op1=ALU.min,
                                           accum_out=nmax[:, h:h + 1]).then_inc(sg["masked"], 1)

            def s_recip(b, g):
                wait(dve, "expd", b, GRP * (g + 1))
                v.reciprocal(rinv[:, GRP * g:GRP * (g + 1)], ssum[:, GRP * g:GRP * (g + 1)]).then_inc(sg["rsum"], 1)

            def s_x1_out(b, _):
                wait(dve, "o_ps", b, 1)
                wait(dve, "xres", b, 1)
                wait(dve, "x1r", b, 0)
                v.tensor_tensor(x1[:], A[0][:, 0:D], xres[:], ALU.add).then_inc(sg["x1"], 1)

            def k_ln_stats(b, _):
                wait(dve, "x1", b, 1)
                ln_stats(b, x1, st2, mv2, 2)

            def rope_cross(b, n):
                bias = 2 * (1 - n)
                tab = ("xk_cos", "xk_sin") if n == 0 else ("xq_cos", "xq_sin")
                wait(dve, "xproj", b, (1, 3)[n])
                if n:
                    wait(dve, "xr_sum", b, 1)
                for m, dst in enumerate((xr_a, xr_b)):
                    v.scalar_tensor_tensor(out=dst[:], in0=Bk[n][:, m * T:(m + 1) * T], scalar=colb[:, bias + m:bias + m + 1],
                                           in1=c(tab[m]), op0=ALU.add, op1=ALU.mult).then_inc(sg["xr_mul"], 1)
                wait(dve, "xr_mul", b, 2 * n + 2)
                v.tensor_tensor(xr[:, n, :], xr_a[:], xr_b[:], ALU.add).then_inc(sg["xr_sum"], 1)
                wait(dve, "xr_sum", b, n + 1)
                v.tensor_copy(xhl[:, n, 0, :], xr[:, n, :]).then_inc(sg["xr_hi"], 1)
                wait(dve, "xr_hi", b, n + 1)
                v.tensor_tensor(xhl[:, n, 1, :], xr[:, n, :], xhl[:, n, 0, :], ALU.subtract).then_inc(sg["xr_lo"], 1)

            def k_v_out(b, _):
                wait(dve, "xproj", b, 2)
                v.tensor_tensor(vaug[:, :, :, 0:XC], Bk[1][:, 0:TB * P].rearrange("p (m h c) -> p m h c", m=TB, c=XC),
                                rowb[:, R_XBV:R_XBV + P].rearrange("p (o h c) -> p o h c", o=1, c=XC).to_broadcast([P, TB, XH, XC]),
                                ALU.add).then_inc(sg["xv"], 1)

            def k_zero_k(b, _):
                wait(dve, "kst", b, 2)
                for j in range(XJ):
                    r = slice(32 * j, 32 * j + 32)
                    v.tensor_copy(kz[r, :, j, :], kst[r, :, :]).then_inc(sg["kz"], 1)

            def k_max(b, h):
                wait(dve, "nat_ps", b, h + 1)
                v.tensor_reduce(xnm[:, h // XJ, h % XJ, :], scores_bank(h).rearrange("p (m t) -> p m t", m=TB), AX.X,
                                ALU.min).then_inc(sg["xmax"], 1)

            def k_max_pack(b, _):
                wait(dve, "xmax", b, XH)
                for m in range(TB):
                    last = v.tensor_scalar(mt[:, m, :, :].rearrange("p g (j r) -> p g j r", r=32)[:, :, :, MROW], xnm[:, :, :, m],
                                           -1.0 / MSCALE, None, ALU.mult)
                last.then_inc(sg["mt"], 1)

            def k_add_max(b, _):
                wait(dve, "mrow", b, 1)
                v.tensor_tensor(qaug[:], qst[:], mrow[:], ALU.add).then_inc(sg["qaug"], 1)

            def c_recip(b, hg):
                wait(dve, "bc_ps", b, hg + 1)
                if hg >= 2:
                    wait(dve, "onorm", b, hg - 1)
                v.reciprocal(bcs[:, hg % 2, :], Bk[hg % 2][:, T:2 * T]).then_inc(sg["bc"], 1)

            def c_x2_out(b, _):
                wait(dve, "wo_ps", b, 1)
                wait(dve, "x1r", b, 1)
                v.tensor_tensor(x2[:], Bk[0][:, 0:T], x1r[:], ALU.add).then_inc(sg["x2"], 1)

            def f_ln_stats(b, _):
                wait(dve, "x2", b, 1)
                ln_stats(b, x2, st3, mv3, 3)

            def f_low_x(b, _):
                wait(dve, "x3h", b, 1)
                v.tensor_tensor(x3[:, 1], Bk[3][:, 0:D].rearrange("p (k s) -> p k s", k=KD), x3[:, 0], ALU.subtract).then_inc(sg["x3l"], 1)

            def f_act(b, n):
                u, g = Bk[2 + n % 2][:, 0:256], Bk[2 + n % 2][:, 256:512]
                wait(dve, "ftanh", b, n + 1)
                v.scalar_tensor_tensor(out=fe[:, n, :], in0=fe[:, n, :], scalar=1.0, in1=u, op0=ALU.add, op1=ALU.mult).then_inc(sg["fact"], 1)
                wait(dve, "fact", b, n + 1)
                v.scalar_tensor_tensor(out=fe[:, n, :], in0=fe[:, n, :], scalar=HS, in1=g, op0=ALU.mult, op1=ALU.mult).then_inc(sg["fhid"], 1)

            def f_low(b, n):
                wait(dve, "fh", b, n + 1)
                v.tensor_tensor(hid[:, 1, 2 * n:2 * n + 2, :], fe[:, n, :].rearrange("p (e s) -> p e s", s=P),
                                hid[:, 0, 2 * n:2 * n + 2, :], ALU.subtract).then_inc(sg["fl"], 1)

            def f_out(b, _):
                wait(dve, "dn_ps", b, 1)
                dve.wait_ge(out_free, b + 1)
                v.scalar_tensor_tensor(out=outt[:], in0=Bk[2][:, 0:D], scalar=small[:, 16:17], in1=x2[:],
                                       op0=ALU.mult, op1=ALU.add).then_inc(sg["outt"], 1)

            def weights(_, n):
                if n == 0:
                    dve.wait_ge(d_mask, 32)
                    v.tensor_scalar(nbn[:].rearrange("p m t -> p (m t)"), maskn, 0.0, None, ALU.is_equal).then_inc(nbs, 1)
                    v.tensor_scalar(nbt[:].rearrange("p m t -> p (m t)"), maskt, 0.0, None, ALU.is_equal).then_inc(nbs, 1)
                    for m, s in enumerate((HUGE, -HUGE)):
                        v.tensor_scalar(bigi[:, m, :], ident, s, None, ALU.mult).then_inc(nbs, 1)
                    dve.wait_ge(nbs, 4)
                    v.tensor_reduce(small[:, 3:4], nbn[:], AX.XY, ALU.max).then_inc(ffsum, 1)
                elif n == 2:
                    dve.wait_ge(totals, 1)
                    v.tensor_scalar(small[:, 4:7], Bk[0][:, 0:3], 1.0 / (D * E), EPS_Q, ALU.mult, ALU.add).then_inc(scales, 1)
                    v.tensor_copy(flag[:], Bk[0][:, 3:4]).then_inc(flagged, 1)
                    dve.wait_ge(scales, 1)
                    v.tensor_scalar(small[:, 8:11], small[:, 4:7], 0.5, None, ALU.mult).then_inc(scales, 1)
                    v.tensor_scalar(small[:, 12:15], small[:, 4:7], -0.5, None, ALU.mult).then_inc(scales, 1)
                    v.tensor_scalar(small[:, 18:19], small[:, 4:5], 0.5, None, ALU.mult).then_inc(scales, 1)
                    v.tensor_tensor(small[:, 17:18], small[:, 4:5], small[:, 5:6], ALU.mult).then_inc(scales, 1)
                    dve.wait_ge(scales, 5)
                    v.scalar_tensor_tensor(out=small[:, 16:17], in0=small[:, 17:18], scalar=0.5 / HS, in1=small[:, 6:7],
                                           op0=ALU.mult, op1=ALU.mult).then_inc(scales, 1)
                for w in {2: (1,), 3: (2,), 4: (0,)}.get(n, ()):
                    v.tensor_scalar(tern[:, w, :], ffw[:, w, :], small[:, 12 + w:13 + w], None, ALU.is_lt).then_inc(scales, 1)
                    dve.wait_ge(scales, 5 + n)
                    v.scalar_tensor_tensor(out=tern[:, w, :], in0=ffw[:, w, :], scalar=small[:, 8 + w:9 + w], in1=tern[:, w, :],
                                           op0=ALU.is_gt, op1=ALU.subtract).then_inc(terns, 1)

            v.memset(ones[:], 1.0).then_inc(zeroed, 1)
            v.memset(half[:], -0.5).then_inc(pool_set, 1)
            v.memset(mt[:], 0.0).then_inc(zeroed, 1)
            v.memset(kz[:], 0.0).then_inc(zeroed, 1)
            v.memset(vaug[:], 0.0).then_inc(zeroed, 1)
            dve.wait_ge(zeroed, 4)
            v.memset(vaug[:, :, :, XC:2 * XC], 1.0).then_inc(zeroed, 1)
            dve.wait_ge(zeroed, 5)
            dve.wait_ge(d_const, 32)
            dve.wait_ge(d_row, 32)
            kw = rowb[:, R_KW:R_KW + NH].rearrange("p (h o) -> p h o", o=1).to_broadcast([P, NH, HD])
            for dst, name in ((cq, "cos"), (sq, "sin")):
                tab = c(name).rearrange("p (o d) -> p o d", o=1).to_broadcast([P, NH, HD])
                v.scalar_tensor_tensor(out=dst[:], in0=tab, scalar=-float(HD) ** -0.5, in1=kw, op0=ALU.mult, op1=ALU.mult).then_inc(tabs, 1)
            dve.wait_ge(tabs, 2)
            n_rb = 0
            for r in range(5):
                at = R_K if r == 0 else R_Q + 512 * (r - 1)
                for ins in rotate(r, rowb[:, at:at + 512], rot[:, 0, :], rot_b[:, 0, :]):
                    ins.then_inc(rbs, 1)
                    n_rb += 1
                dve.wait_ge(rbs, n_rb)
                v.tensor_tensor(rowb[:, at:at + 512], rot[:, 0, :], rot_b[:, 0, :], ALU.add).then_inc(rbs, 1)
                n_rb += 1
                dve.wait_ge(rbs, n_rb)
            steps = dict(
                S=dict(ln_stats=s_ln_stats, ln_apply=lambda b, _: ln_apply(b, x_sb, mv1, rs1, xn1, 1), rope=s_rope, v_out=s_v_out,
                       low=s_low, mask=s_mask, recip=s_recip, x1_out=s_x1_out),
                K=dict(ln_stats=k_ln_stats, ln_apply=lambda b, _: ln_apply(b, x1, mv2, rs2, xn2, 2),
                       rope_k=lambda b, _: rope_cross(b, 0), rope_q=lambda b, _: rope_cross(b, 1), v_out=k_v_out, zero_k=k_zero_k,
                       max=k_max, max_pack=k_max_pack, add_max=k_add_max),
                C=dict(recip=c_recip, x2_out=c_x2_out),
                F=dict(ln_stats=f_ln_stats, ln_apply=lambda b, _: ln_apply(b, x2, mv3, rs3, xn3, 3), low_x=f_low_x, act=f_act,
                       low=f_low, out=f_out),
                W=dict(weights=weights))
            run(steps, first_steps(), S=0, W=0)
            dve.wait_ge(terns, 3)
            rounds(dve, steps)

        @block.scalar
        def _(act):
            a = nc.scalar
            act.dma_start(rowb[:], rows.to_broadcast([P, WROW])).then_inc(d_row, 16)
            act.dma_start(colb[:], cols).then_inc(d_row, 16)
            act.dma_start(k16[:], c16).then_inc(d_const, 16)
            act.dma_start(maskn, mask_n).then_inc(d_mask, 16)
            act.dma_start(maskt, mask_t).then_inc(d_mask, 16)
            act.dma_start(ffw[:, 1, :], w_gate).then_inc(d_ffw[1], 16)
            act.dma_start(ffw[:, 2, :], w_down).then_inc(d_ffw[2], 16)
            act.dma_start(xw_sb[:], xw).then_inc(d_x, 16)
            act.dma_start(xwo_sb[:], xwo).then_inc(d_x, 16)

            def weights(_, n):
                if n == 0:
                    act.wait_ge(nbs, 2)
                    act.dma_start(ffw[:, 0, :], w_up).then_inc(d_ffw[0], 16)
                for w in {0: (1,), 1: (2, 0)}.get(n, ()):
                    act.wait_ge(d_ffw[w], 16)
                    a.activation(tern[:, w, :], ffw[:, w, :], ACT.Abs, accum_out=small[:, w:w + 1]).then_inc(ffsum, 1)

            def s_transpose_x(b, _):
                wait(act, "xnT_ps", b, 1)
                a.copy(xnT[:].rearrange("p k s -> p (k s)"), A[2][:, 0:D]).then_inc(sg["xnT"], 1)

            def s_high(b, r):
                wait(act, "roped", b, r + 1)
                dst = ks[:, :, 0] if r == 0 else qs[:, (r - 1) % 2]
                if r >= 3:
                    wait(act, "qkT_ps", b, r)
                a.copy(dst[:, :, 0, :], rot[:, r % 2, :].rearrange("p (h d) -> p h d", d=HD)).then_inc(sg["hi"], 1)

            def s_transpose(b, n):
                wait(act, "qkT_ps", b, n + 1)
                dst = kT[:, 4 * n:4 * n + 4].rearrange("p g v s -> p (g v s)") if n < 2 else \
                    qT[:, 8 * (n - 2):8 * (n - 1)].rearrange("p h s -> p (h s)")
                a.copy(dst, A[2].bitcast(F16)).then_inc(sg["qkT"], 1)

            def s_exp(b, g):
                if g >= 2:
                    wait(act, "pT_ps", b, g - 1)
                for j in range(GRP):
                    h = GRP * g + j
                    wait(act, "masked", b, h + 1)
                    a.activation(ex[:, g % 2, j, :], sm[:, g % 2, j, :], ACT.Exp, bias=nmax[:, h:h + 1], scale=-1.0,
                                 accum_out=ssum[:, h:h + 1]).then_inc(sg["expd"], 1)

            def s_copy_p(b, g):
                wait(act, "pT_ps", b, g + 1)
                if g >= 2:
                    wait(act, "pv", b, g - 1)
                a.copy(pT[:, g % 2, :], A[2]).then_inc(sg["pT"], 1)

            def s_o_out(b, n):
                wait(act, "pv", b, 2 * n + 2)
                a.copy(oT[:, n].rearrange("p j s -> p (j s)"), A[3]).then_inc(sg["oT"], 1)

            def k_spread(b, n):
                wait(act, "sel_ps", b, n + 1)
                m = n % 2
                dst = (kst, qst)[n // 2][:, 2 * m:2 * m + 2, :].rearrange("p g t -> p (g t)")
                if n < 2:
                    a.activation(dst, Bk[m], ACT.Identity, bias=c("kcol")).then_inc(sg["kst"], 1)
                else:
                    a.copy(dst, Bk[m]).then_inc(sg["qst"], 1)

            def k_max_transpose(b, _):
                wait(act, "mt_ps", b, 1)
                a.copy(mrow[:].rearrange("p g t -> p (g t)"), Bk[2].bitcast(F16)).then_inc(sg["mrow"], 1)

            def c_exp(b, h):
                wait(act, "st_ps", b, h + 1)
                if h >= 2:
                    wait(act, "xpv", b, h - 1)
                a.activation(ffw[:, 0, 512 * (h % 2):512 * (h % 2) + 512], Bk[2 + h % 2], ACT.Exp, scale=-1.0).then_inc(sg["xexp"], 1)

            def c_out(b, hg):
                wait(act, "xpv", b, XJ * (hg + 1))
                a.copy(oraw[:, hg, :], Bk[hg % 2][:, 0:T]).then_inc(sg["oraw"], 1)

            def f_transpose_x(b, _):
                wait(act, "x3T_ps", b, 1)
                a.copy(x3[:, 0], Bk[3][:, 0:D].rearrange("p (k s) -> p k s", k=KD)).then_inc(sg["x3h"], 1)

            def f_tanh(b, n):
                wait(act, "ff_ps", b, n + 1)
                a.activation(fe[:, n, :], Bk[2 + n % 2][:, 0:256], ACT.Tanh, scale=small[:, 18:19]).then_inc(sg["ftanh"], 1)

            def f_high(b, n):
                wait(act, "fhid", b, n + 1)
                a.copy(hid[:, 0, 2 * n:2 * n + 2, :], fe[:, n, :].rearrange("p (e s) -> p e s", s=P)).then_inc(sg["fh"], 1)

            steps = dict(
                S=dict(transpose_x=s_transpose_x, high=s_high, transpose=s_transpose, exp=s_exp, copy_p=s_copy_p, o_out=s_o_out),
                K=dict(spread=k_spread, max_transpose=k_max_transpose),
                C=dict(exp=c_exp, out=c_out),
                F=dict(transpose_x=f_transpose_x, tanh=f_tanh, high=f_high),
                W=dict(weights=weights))
            run(steps, first_steps(), S=0, W=0)
            act.wait_ge(scales, 4)
            rounds(act, steps)

        @block.gpsimd
        def _(pool):
            g_ = nc.gpsimd
            pool.wait_ge(pool_set, 1)
            pool.wait_ge(d_row, 32)
            pool.wait_ge(zeroed, 1)

            def power(b, mv, rs, n):
                wait(pool, f"ln{n}", b, 3)
                g_.tensor_tensor(rs[:], mv[:, 2:3], half[:], ALU.pow).then_inc(sg[f"rstd{n}"], 1)

            def s_ln_stats(b, _):
                power(b, mv1, rs1, 1)

            def s_ln_apply(b, _):
                pool.wait_ge(x_in, b * 16 + 16)
                wait(pool, "x1", b, 0)
                g_.tensor_tensor(xres[:], x_sb[:], rowb[:, R_BO:R_BO + D], ALU.add).then_inc(sg["xres"], 1)

            def s_bias(b, r):
                wait(pool, "rope_mul", b, 2 * r + 2)
                at = R_K if r == 0 else R_Q + 512 * (r - 1)
                g_.tensor_tensor(rot_b[:, r % 2, :], rot_b[:, r % 2, :], rowb[:, at:at + 512], ALU.add).then_inc(sg["biased"], 1)
                wait(pool, "biased", b, r + 1)
                g_.tensor_tensor(rot[:, r % 2, :], rot[:, r % 2, :], rot_b[:, r % 2, :], ALU.add).then_inc(sg["roped"], 1)

            def s_recip(b, g):
                wait(pool, "rsum", b, g + 1)
                r = rinv[:, GRP * g:GRP * (g + 1)].rearrange("p (j o) -> p j o", o=1).to_broadcast([P, GRP, P])
                g_.tensor_tensor(ex[:, g % 2], ex[:, g % 2], r, ALU.mult).then_inc(sg["normed"], 1)

            def k_keep(b, _):
                wait(pool, "x1", b, 1)
                wait(pool, "x2", b, 0)
                g_.tensor_tensor(x1r[:], x1[:], colb[:, 4:5].to_broadcast([P, D]), ALU.add).then_inc(sg["x1r"], 1)

            def c_scale(b, hg):
                wait(pool, "bc", b, hg + 1)
                g_.tensor_tensor(oraw[:, hg, :], oraw[:, hg, :], bcs[:, hg % 2, :], ALU.mult).then_inc(sg["onorm"], 1)

            steps = dict(
                S=dict(ln_stats=s_ln_stats, ln_apply=s_ln_apply, bias=s_bias, recip=s_recip),
                K=dict(ln_stats=lambda b, _: power(b, mv2, rs2, 2), keep=k_keep),
                C=dict(scale=c_scale),
                F=dict(ln_stats=lambda b, _: power(b, mv3, rs3, 3)),
                W={})
            run(steps, first_steps(), S=0, W=0)
            pool.wait_ge(terns, 3)
            rounds(pool, steps)


def constants():
    f = np.float32
    c32 = np.zeros((P, W32), f)

    def put(name, a):
        c32[:, C32[name][0]:C32[name][1]] = a

    put("ident", np.eye(P, dtype=f))
    s = np.arange(P)
    put("causal", np.where(s[None, :] > s[:, None], f(BIG), f(0)))
    inv = (f(1) / f(10000.0) ** (np.arange(0, HD, 2, dtype=f) / f(HD))).astype(f)
    ang = np.arange(S, dtype=f)[:, None] * inv[None, :]
    put("cos", np.concatenate([np.cos(ang), np.cos(ang)], 1))
    put("sin", np.concatenate([-np.sin(ang), np.sin(ang)], 1))
    rd = XC // 2
    th = (f(1) / f(10000.0) ** (np.arange(0, rd, 2, dtype=f) / f(rd))).astype(f)
    ang = (np.arange(T, dtype=f)[:, None] * th[None, :]).T
    cosx, sinx = np.ones((XC, T), f), np.zeros((XC, T), f)
    cosx[0:2], cosx[2:4] = np.cos(ang), np.cos(ang)
    sinx[0:2], sinx[2:4] = -np.sin(ang), np.sin(ang)
    cosx, sinx = np.tile(cosx, (XH, 1)), np.tile(sinx, (XH, 1))
    put("xk_cos", cosx)
    put("xk_sin", sinx)
    scale = f(-1.0 / np.sqrt(XC))
    put("xq_cos", cosx * scale)
    put("xq_sin", sinx * scale)
    row = np.arange(P)
    put("kcol", np.where(row % 32 == MROW, f(MSCALE), f(0))[:, None])
    put("selsum", np.where(row[:, None] == 32 * (row[None, :] // 32) + XC, f(1), f(0)))
    c16 = np.zeros((P, W16), np.float16)
    c16[:, 0:P] = np.eye(P)
    c16[:, P:2 * P] = 10000.0 * np.eye(P)
    for name, slots in (("k_hi", (0, 2)), ("k_lo", (1,)), ("q_hi", (0, 1)), ("q_lo", (2,))):
        for hg in range(XG):
            for j in range(XJ):
                for r in slots:
                    for d in range(XC):
                        c16[(hg * XJ + j) * XC + d, C16[name][0] + hg * P + 32 * j + XC * r + d] = 1.0
    return c32, c16


def kernel(**inputs):
    import concourse.bacc as bacc
    from concourse.bass_utils import run_bass_kernel_spmd

    a = {k: np.asarray(v) for k, v in inputs.items()}

    def tiles(w):
        k, n = w.shape
        return w.reshape(k // P, P, n).transpose(1, 0, 2)

    wq, wk, wv = a["L0_attn_Wq"].T, a["L0_attn_Wk"].T, a["L0_attn_Wv"].T
    perm = np.arange(P).reshape(XH, XC)[:, [2, 3, 0, 1, 4, 5, 6, 7]].ravel()
    xwq, xwk, xwv = a["L0_xattn_wq"], a["L0_xattn_wk"], a["L0_xattn_wv"]
    xbq, xbk = a["L0_xattn_bq"], a["L0_xattn_bk"]
    xwo = np.zeros((XJ, 32, XG, P), np.float32)
    xwo[:, 0:XC] = a["L0_xattn_wo"].T.reshape(XG, XJ, XC, P).transpose(1, 2, 0, 3)
    mask = a["mask_1x1x2048x2048_if1"].reshape(T, T)
    c32, c16 = constants()
    arrays = dict(
        x=a["x"], ctx=a["ctx_2048"],
        mask_n=mask.reshape(TB, P, T).transpose(1, 0, 2).reshape(P, TB * T),
        mask_t=mask.T.reshape(TB, P, T).transpose(1, 0, 2).reshape(P, TB * T),
        w_qkv=tiles(np.concatenate([wk, wv, wq], 1)),
        w_o=a["L0_attn_Wo"].T.reshape(NPAIR, 2, GRP, HD, D).transpose(1, 3, 0, 2, 4).reshape(P, NPAIR, GRP, D),
        rows=np.concatenate([a["L0_attn_bk"], a["L0_attn_bv"], a["L0_attn_bq"], a["L0_attn_bo"], a["L0_xattn_bv"],
                             a["L0_attn_key_weights"]])[None],
        cols=np.stack([xbq, xbq[perm], xbk, xbk[perm], a["L0_xattn_bo"]], 1),
        xw=np.stack([xwq.T, xwq[perm].T, xwk.T, xwk[perm].T, xwv.T], 1),
        xwo=xwo.reshape(P, XG, P),
        w_up=tiles(a["L0_ffn_W_up"].T).reshape(P, KD * E),
        w_gate=tiles(a["L0_ffn_W_gate"].T).reshape(P, KD * E),
        w_down=tiles(a["L0_ffn_W_down"].T).reshape(P, ET * D),
        c32=c32, c16=c16)
    arrays = {k: np.ascontiguousarray(v) for k, v in arrays.items()}
    nc = bacc.Bacc("TRN2", target_bir_lowering=False, num_devices=1)
    aps = {k: nc.dram_tensor(f"in_{k}", v.shape, mybir.dt.from_np(v.dtype), kind="ExternalInput").ap() for k, v in arrays.items()}
    out = nc.dram_tensor("out_0", (B, S, D), F32, kind="ExternalOutput").ap()
    build(nc, *aps.values(), out)
    r = run_bass_kernel_spmd(nc, [{f"in_{k}": v for k, v in arrays.items()}], core_ids=[0])
    return r.results[0]["out_0"]
```

```python
from contextlib import ExitStack

import numpy as np
import concourse.bass as bass
from concourse import mybir

F32 = mybir.dt.float32
F16 = mybir.dt.float16
BF16 = mybir.dt.bfloat16
I32 = mybir.dt.int32
ALU = mybir.AluOpType
ACT = mybir.ActivationFunctionType
AX = mybir.AxisListType

B, S, D = 8, 128, 256
P = 128
KD = D // P
NH, NKV, HD = 32, 8, 64
GRP = NH // NKV
NPAIR = NKV // 2
XH, XC, XG = 16, 8, 4
XJ = XH // XG
T = D
TB = T // P
E = 1024
ET = E // P
NF = ET // 2
BIG = 1.0e30
NCH = (NH + 2 * NKV) * HD // 512
WS = 64.0
MROW, MSCALE = 24, 256.0
HS = 1.0 / 32
EPS_LN, EPS_Q = 1e-5, 1e-8
HUGE = 2.0 ** 100

C32 = {}
_at = 0
for _n, _w in (("ident", P), ("causal", P), ("cos", HD), ("sin", HD), ("xk_cos", T), ("xk_sin", T),
               ("xq_cos", T), ("xq_sin", T), ("kcol", 1), ("selsum", P)):
    C32[_n] = (_at, _at + _w)
    _at += _w
W32 = _at
W32_FIRST = C32["xk_cos"][0]
C16 = {"ident": (0, P), "ten": (P, 2 * P), "k_hi": (256, 768), "k_lo": (768, 1280), "q_hi": (1280, 1792), "q_lo": (1792, 2304)}
W16 = 2304
NQKV = (NH + 2 * NKV) * HD
R_KW, R_K = 0, NH
R_V = R_K + NKV * HD
R_BO = R_V + NKV * HD
R_Q = R_BO + D
R_XBV = R_Q + NH * HD
WROW = R_XBV + P

SELF_SIGNALS = dict(
    ln1=3, rstd1=1, xn1=1, xres=1, xnT_ps=1, xnT=1, xnTl=1,
    qkv_ps=6, rope_mul=10, biased=5, roped=5, hi=5, lo=5, kswap=1, v_sb=1,
    qkT_ps=6, qkT=6, s_ps=8, masked=32, expd=32, rsum=8, normed=8, pT_ps=8, pT=8, pv=8, oT=4, oTl=4, o_ps=1, x1=1)
CROSS_SIGNALS = dict(
    ln2=3, rstd2=1, xn2=1, xproj=3, xr_mul=4, xr_sum=2, xr_hi=2, xr_lo=2, xv=1, sel_ps=4, kst=2, qst=2, kz=4,
    nat_ps=16, xmax=16, mt=1, mt_ps=1, mrow=1, qaug=1, st_ps=16, xexp=16, xpv=16, oraw=4, bc_ps=4, bc=4, onorm=4,
    wo_ps=1, x1r=1, x2=1)
FFN_SIGNALS = dict(
    ln3=3, rstd3=1, xn3=1, x3T_ps=1, x3h=1, x3l=1,
    ff_ps=NF, ftanh=NF, fact=NF, fhid=NF, fh=NF, fl=NF, dn_ps=1, outt=1)


ORDER = """
S.qkv1 C.exp0 C.exp1 S.qkv2 S.rope1 S.keep_x C.transposed0 C.transposed1 S.rope2 S.qkv3 C.pv0 C.exp2 C.transposed2
C.exp3 C.transposed3 C.exp4 C.exp5 S.high1 C.pv1 S.bias1 S.bias2 C.out0 S.transpose0 S.v_out S.low1 Q.ln_stats C.pv2
C.transposed4 C.transposed5 C.exp6 C.pv3 S.qkv4 C.transposed6 C.transposed7 S.low2 C.exp7 C.scale0 S.high2 C.pv4 C.pv5
C.sums0 C.exp8 C.exp9 S.bias3 S.bias4 C.scale1 C.scale2 S.transpose1 S.low3 C.out1 K.ln_stats C.transposed8 C.pv6
C.pv7 C.exp10 C.exp11 C.recip0 S.rope3 C.transposed9 C.exp12 S.qkv5 C.exp13 S.rope4 C.out2 C.recip1 C.recip2 C.pv8
C.transposed10 C.transposed11 C.scale3 C.pv9 C.sums1 S.mask0 C.transposed12 C.pv10 C.pv11 C.transposed13 S.transpose2
C.transposed14 C.transposed15 C.recip3 C.exp14 C.exp15 S.high3 C.pv12 Q.ln_apply C.out3 C.sums2 K.ln_apply C.pv13
S.scores0 C.pv14 C.pv15 S.mask1 S.mask2 S.transpose3 S.exp0 C.sums3 S.scores1 S.scores2 S.high4 S.transpose4 S.exp1
C.wo S.low4 S.transpose5 S.recip0 C.x2_out S.recip1 F.ln_stats S.copy_p0 S.mask3 S.scores3 S.exp2 K.proj_k
S.transpose_p0 K.rope_k K.proj_v S.scores4 S.pv0 S.copy_p1 S.transpose_p1 K.v_out F.ln_apply S.recip2 S.mask4
K.spread0 K.keep K.proj_q K.rope_q F.transpose_x S.exp3 S.copy_p2 S.pv1 S.transpose_p2 K.spread1 F.low_x S.o_out0
S.recip3 S.scores5 F.up_gate0 K.spread2 F.tanh0 K.spread3 S.mask5 S.transpose_p3 S.scores6 K.zero_k S.scores7 S.low_o0
F.act0 S.recip4 S.exp4 K.max0 S.copy_p3 F.act1 S.mask6 S.mask7 F.tanh1 S.exp5 K.scores0 F.up_gate1 S.recip5 S.pv2
S.pv3 F.act2 K.max1 F.up_gate2 F.tanh2 F.low0 F.act3 Q.low_xn F.low1 F.low2 F.low3 F.high0 K.max2 F.up_gate3 S.recip6
K.max3 F.tanh3 S.transpose_p4 S.low_o1 K.scores1 F.high1 K.scores2 S.copy_p4 Q.transpose_x S.wo0 S.exp6 K.scores3
Q.rope S.transpose_p5 S.recip7 Q.qkv F.down K.scores4 K.scores5 F.high2 F.high3 F.out K.max4 S.transpose_p6 K.max5
K.max6 S.o_out1 K.max7 K.max8 S.pv4 S.low_o2 K.scores6 K.max9 K.max10 K.max11 S.exp7 S.copy_p5 S.pv5 K.max12 K.scores7
K.scores8 K.scores9 S.transpose_p7 S.wo1 K.scores10 K.scores11 S.low_o3 S.pv6 S.pv7 Q.bias K.scores12 S.copy_p6
K.max13 K.max14 K.max15 S.o_out2 K.max_pack S.copy_p7 S.x1_out K.scores13 K.scores14 Q.low S.o_out3 K.scores15 S.wo2
S.wo3 Q.high K.add_max K.max_transpose
"""


def parsed(word):
    chain, step = word.split(".")
    name = step.rstrip("0123456789")
    return chain, name, int(step[len(name):] or 0)


BODY = [parsed(word) for word in ORDER.split()]


def steps_of(chains):
    return [step for step in BODY if step[0] in chains]


FIRST = [parsed(word) for word in """
S.transpose_x S.ln_stats S.bias0 S.bias1 S.ln_apply S.low_xn S.qkv0 W.high_w0 W.low_w0 W.turn0 S.rope0 S.high0
W.tables W.high_w1 W.low_w1 W.high_w2 S.low0 S.low1 S.qkv1 S.qkv2 S.keep_x W.low_w2 W.turn1 S.rope1 W.high_w3
S.transpose0 S.transpose1 S.v_out W.low_w3 W.turn2 W.high_w4 S.rope2 S.bias2 W.low_w4 S.bias3 W.turn3 W.high_w5 S.qkv3
S.rope3 S.high1 S.high2 S.transpose2 W.low_w5 S.high3 S.qkv4 S.qkv5 S.scores0 W.masks S.low2 W.turn4 S.low3 S.rope4
S.mask0 S.mask1 S.bias4 W.high_o0 S.transpose3 W.low_o0 W.high_o1 S.transpose4 S.exp0 S.scores1 S.high4 S.exp1
S.transpose5 S.copy_p0 S.low4 S.scores2 S.transpose_p0 S.scores3 S.recip0 S.recip1 S.mask2 S.exp2 S.copy_p1
S.transpose_p1 S.scores4 W.low_o1 S.mask3 S.mask4 S.recip2 S.recip3 W.sums0 S.pv0 S.transpose_p2 S.exp3 S.copy_p2
S.exp4 Q.ln_stats S.o_out0 S.scores5 S.scores6 S.copy_p3 S.mask5 S.mask6 S.pv1 Q.ln_apply S.exp5 S.recip4 S.low_o0
S.transpose_p3 Q.transpose_x S.scores7 S.pv2 S.transpose_p4 Q.low_xn W.sums1 S.o_out1 S.mask7 S.pv3 Q.qkv W.sums2
S.copy_p4 W.totals S.low_o1 S.transpose_p5 S.exp6 S.exp7 S.wo0 S.recip5 S.wo1 S.pv4 S.pv5 S.copy_p5 Q.rope W.scales
W.ternary0 S.recip6 S.recip7 S.o_out2 S.transpose_p6 S.transpose_p7 S.low_o2 S.pv6 W.ternary1 S.pv7 Q.bias S.low_o3
S.copy_p6 S.copy_p7 Q.low S.x1_out W.ternary2 S.o_out3 S.wo2 Q.high S.wo3
""".split()]

END = [parsed(word) for word in """
K.proj_k K.rope_k C.transposed0 C.exp0 C.exp1 C.exp2 C.transposed1 C.transposed2 C.exp3 C.exp4 C.out0 C.pv0 C.exp5
C.exp6 C.transposed3 C.pv1 K.proj_v C.pv2 C.transposed4 C.pv3 C.transposed5 K.ln_stats C.pv4 C.exp7 C.transposed6
C.sums0 C.exp8 C.transposed7 C.pv5 C.scale0 C.pv6 C.transposed8 C.pv7 C.transposed9 C.transposed10 C.pv8 C.scale1
C.out1 C.scale2 C.scale3 C.exp9 C.exp10 K.ln_apply C.exp11 C.sums1 C.exp12 C.transposed11 C.pv9 C.recip0 C.pv10
C.transposed12 C.pv11 C.out2 C.transposed13 C.exp13 C.transposed14 C.recip1 C.recip2 C.sums2 C.transposed15 C.exp14
C.pv12 K.proj_q C.exp15 C.pv13 C.pv14 K.rope_q K.spread0 C.pv15 K.spread1 C.out3 K.spread2 K.v_out K.zero_k C.recip3
K.spread3 K.max0 C.sums3 K.max1 K.max2 C.x2_out K.max3 F.ln_stats K.max4 K.max5 K.scores0 K.scores1 K.scores2
F.ln_apply K.max6 K.max7 F.low_x K.max8 K.max9 C.wo K.scores3 K.scores4 K.scores5 K.scores6 K.scores7 K.scores8
F.transpose_x K.scores9 K.scores10 K.max10 K.scores11 F.act0 F.act1 F.tanh0 K.max11 F.tanh1 K.max12 K.max13 F.up_gate0
F.up_gate1 F.up_gate2 K.keep K.scores12 K.scores13 F.act2 K.max14 K.max15 F.act3 K.max_pack F.tanh2 F.tanh3 K.scores14
K.scores15 F.low0 F.up_gate3 F.low1 F.high0 F.high1 F.low2 F.high2 F.high3 F.low3 K.max_transpose K.add_max F.down
F.out
""".split()]

LAST = [parsed(word) for word in """
C.exp0 C.transposed0 C.exp1 C.exp2 C.transposed1 C.exp3 C.transposed2 C.exp4 C.pv0 C.transposed3 C.out0 C.pv1 C.pv2
C.transposed4 C.pv3 C.transposed5 C.pv4 C.recip0 C.recip1 C.transposed6 C.sums0 C.scale0 C.transposed7 C.pv5
C.transposed8 C.exp5 C.exp6 C.pv6 C.pv7 C.transposed9 C.transposed10 C.scale1 C.pv8 C.exp7 C.exp8 C.out1 C.exp9
C.sums1 C.scale2 C.scale3 C.recip2 C.pv9 C.transposed11 C.recip3 C.x2_out C.pv10 C.transposed12 C.transposed13 C.pv11
F.ln_stats C.transposed14 C.exp10 C.pv12 C.pv13 F.ln_apply C.exp11 F.low_x C.exp12 C.exp13 F.act0 C.out2
C.transposed15 C.sums2 C.exp14 C.exp15 F.act1 C.pv14 C.pv15 C.sums3 C.wo C.out3 F.transpose_x F.up_gate0 F.up_gate1
F.low0 F.act2 F.act3 F.low1 F.up_gate2 F.up_gate3 F.tanh0 F.tanh1 F.high0 F.tanh2 F.down F.tanh3 F.high1 F.high2
F.high3 F.low2 F.low3 F.out
""".split()]


def build(nc, x, ctx, mask_n, mask_t, w_qkv, w_o, rows, cols, xw, xwo, w_up, w_gate, w_down, c32, c16, out):
    with ExitStack() as st:
        def sb(name, shape, dt=F32):
            return st.enter_context(nc.sbuf_tensor(name, shape, dt))

        def sem(name):
            return st.enter_context(nc.semaphore(name))

        k32 = sb("k32", [P, W32])
        k16 = sb("k16", [P, W16], F16)
        rowb = sb("rowb", [P, WROW])
        colb = sb("colb", [P, 5])
        wqkv = sb("wqkv", [P, 2, NCH, KD, 512], F16)
        wo = sb("wo", [P, 2, NPAIR, GRP, D], F16)
        xw_sb = sb("xw_sb", [P, 5, P])
        xwo_sb = sb("xwo_sb", [P, XG, P])
        ffw = sb("ffw", [P, 3, KD * E])
        tern = sb("tern", [P, 3, KD * E], F16)
        cq = sb("cq", [P, NH, HD])
        sq = sb("sq", [P, NH, HD])
        stage = ffw[:].rearrange("p w n -> p (w n)").rearrange("p (c n) -> p c n", c=NCH)
        nbn = sb("nbn", [P, TB, T], F16)
        nbt = sb("nbt", [P, TB, T], F16)
        bigi = sb("bigi", [P, 2, P], BF16)
        small = sb("small", [P, 32])
        flag = sb("flag", [P, 1], I32)
        half = sb("half", [P, 1])
        ones = sb("ones", [P, P])
        ident = k32[:, C32["ident"][0]:C32["ident"][1]]
        ident16 = k16[:, 0:P]

        def c(name):
            return k32[:, C32[name][0]:C32[name][1]]

        x_sb = sb("x_sb", [P, D])
        xres = sb("xres", [P, D])
        xn1 = sb("xn1", [P, D])
        xnT = sb("xnT", [P, 2, KD, P], F16)
        st1, mv1, rs1 = sb("st1", [P, 6]), sb("mv1", [P, 3]), sb("rs1", [P, 1])
        rot_b = sb("rot_b", [P, 2, 512])
        rot = sb("rot", [P, 2, 512])
        qs = sb("qs", [P, 2, 8, 2, HD], F16)
        ks = sb("ks", [P, NKV, 2, 2, HD], F16)
        v_sb = sb("v_sb", [P, NKV * HD])
        qT = sb("qT", [P, NH, P], F16)
        kT = sb("kT", [P, NKV, 2, P], F16)
        sm = sb("sm", [P, 2, GRP, P])
        ex = sb("ex", [P, 2, GRP, P])
        nmax = sb("nmax", [P, NH])
        ssum = sb("ssum", [P, NH])
        rinv = sb("rinv", [P, NH])
        pT = sb("pT", [P, 2, GRP * P])
        oT = sb("oT", [P, 2, NPAIR, GRP, P], F16)
        x1 = sb("x1", [P, D])
        ctx_sb = sb("ctx_sb", [P, D])
        xn2 = sb("xn2", [P, T])
        st2, mv2, rs2 = sb("st2", [P, 6]), sb("mv2", [P, 3]), sb("rs2", [P, 1])
        xr_a = sb("xr_a", [P, T])
        xr_b = sb("xr_b", [P, T])
        xr = sb("xr", [P, 2, T])
        xhl = sb("xhl", [P, 2, 2, T], F16)
        kst = sb("kst", [P, XG, T], F16)
        qst = sb("qst", [P, XG, T], F16)
        maskn = qst[:].rearrange("p g t -> p (g t)").bitcast(I32)
        maskt = xhl[:].rearrange("p n v t -> p (n v t)").bitcast(I32)
        mrow = kst
        qaug = sb("qaug", [P, XG, T], F16)
        kz = sb("kz", [P, XG, XJ, T], F16)
        vaug = sb("vaug", [P, TB, XH, 32])
        xnm = sb("xnm", [P, XG, XJ, TB])
        mt = sb("mt", [P, TB, XG, P], F16)
        xpT = ffw[:, 0, 0:1024].rearrange("p (n m t) -> p n m t", n=2, m=TB)
        oraw = ffw[:, 0, 1024:2048].rearrange("p (g t) -> p g t", g=XG)
        bcs = ffw[:, 2, 0:512].rearrange("p (n t) -> p n t", n=2)
        x2 = ffw[:, 2, 512:768]
        x1r = ffw[:, 2, 1536:1792]
        xn3 = ffw[:, 2, 768:1024]
        st3, mv3, rs3 = sb("st3", [P, 6]), sb("mv3", [P, 3]), sb("rs3", [P, 1])
        x3 = ffw[:, 2, 1024:1280].bitcast(F16).rearrange("p (v k s) -> p v k s", v=2, k=KD)
        fe = ffw[:, 1, 0:1024].rearrange("p (f n) -> p f n", f=NF)
        hid = ffw[:, 1, 1024:2048].bitcast(F16).rearrange("p (v e s) -> p v e s", v=2, e=ET)
        outt = ffw[:, 2, 1280:1536]

        PS = st.enter_context(nc.psum_tensor("PS", [P, 8, 512], F32))
        A = [PS[:, n, :] for n in range(4)]
        Bk = [PS[:, n, :] for n in range(4, 8)]
        QB = (A[0], A[1], A[3])

        def kb(b):
            return A if type(b) is int and b == B - 1 else Bk

        def v_bank(b):
            return A[2] if kb(b) is A else Bk[1]

        def scores_bank(b, h):
            return kb(b)[h % 2 if h < 6 else (h - 4) % 4]

        sg = {n: sem(n) for n in (*SELF_SIGNALS, *CROSS_SIGNALS, *FFN_SIGNALS)}
        per = {**SELF_SIGNALS, **CROSS_SIGNALS, **FFN_SIGNALS}
        x_in, ctx_in, out_st, out_free = sem("x_in"), sem("ctx_in"), sem("out_st"), sem("out_free")
        d_first, d_const, d_row1, d_row, d_x, d_mask = (sem(n) for n in ("d_first", "d_const", "d_row1", "d_row", "d_xw", "d_mask"))
        d_w = [sem(f"d_w{n}") for n in range(NCH)]
        d_wo = [sem(f"d_wo{n}") for n in range(2)]
        w_hi, w_lo, wo_hi, wo_lo = (sem(n) for n in ("w_hi", "w_lo", "wo_hi", "wo_lo"))
        d_ffw = [sem(f"d_ffw{n}") for n in range(3)]
        tabs, turned, ones_set, zeroed, nbs, ffsum, totals, scales, terns, pool_set, flagged = (
            sem(n) for n in ("tabs", "turned", "ones_set", "zeroed", "nbs", "ffsum", "totals", "scales", "terns", "pool_set", "flagged"))
        passed = sem("passed")

        def wait(eng, name, b, k):
            v = b * per[name] + k
            if not (type(v) is int and v <= 0):
                eng.wait_ge(sg[name], v)

        block = st.enter_context(nc.Block())

        def run(steps, order, **batch):
            for chain, name, n in order:
                of = steps["S" if chain == "Q" else chain]
                if name in of:
                    of[name](batch[chain], n)

        def rounds(eng, steps):
            run(steps, steps_of("SKQ"), S=1, K=0, Q=2)
            with eng.Fori(2, B - 1) as i:
                run(steps, BODY, S=i, K=i - 1, C=i - 2, F=i - 2, Q=i + 1)
            run(steps, steps_of("SKCF"), S=B - 1, K=B - 2, C=B - 3, F=B - 3)
            run(steps, END, K=B - 1, C=B - 2, F=B - 2)
            run(steps, LAST, C=B - 1, F=B - 1)

        def tables(r):
            if r == 0:
                return (c(n).rearrange("p (o d) -> p o d", o=1).to_broadcast([P, 8, HD]) for n in ("cos", "sin"))
            return cq[:, 8 * (r - 1):8 * r, :], sq[:, 8 * (r - 1):8 * r, :]

        def factors(r, src, dst, dst_b):
            cos, sin = tables(r)
            halves = [t.rearrange("p (h t d) -> p h t d", t=2, d=HD // 2) for t in (src, dst_b)]
            whole = [t.rearrange("p (h d) -> p h d", d=HD) for t in (src, dst)]
            return (whole[1], whole[0], cos), (halves[1], halves[0][:, :, ::-1, :], sin.rearrange("p h (t d) -> p h t d", t=2))

        def low_part(e, r):
            dst = ks[:, :, 0] if r == 0 else qs[:, (r - 1) % 2]
            return e.tensor_tensor(dst[:, :, 1, :], rot[:, r % 2, :].rearrange("p (h d) -> p h d", d=HD), dst[:, :, 0, :], ALU.subtract)

        @block.sync
        def _(sp):
            sp.sem_inc(out_free, 1)
            sp.dma_start(x_sb[:], x[0]).then_inc(x_in, 16)
            sp.dma_start(k32[:, 0:W32_FIRST], c32[:, 0:W32_FIRST]).then_inc(d_first, 16)
            for n in range(NCH):
                sp.dma_start(stage[:, n, :], w_qkv[:, n, :]).then_inc(d_w[n], 16)
            sp.wait_ge(sg["xn1"], 1)
            sp.wait_ge(sg["xres"], 1)
            sp.dma_start(x_sb[:], x[1]).then_inc(x_in, 16)
            for n in range(2):
                sp.wait_ge(w_lo, 2 * n + 2)
                sp.dma_start(ffw[:, n, :], w_o[:, n, :]).then_inc(d_wo[n], 16)
            sp.wait_ge(w_lo, NCH)
            sp.dma_start(ffw[:, 2, :], w_down).then_inc(d_ffw[2], 16)
            for n, w in enumerate((w_up, w_gate)):
                sp.wait_ge(wo_lo, n + 1)
                sp.dma_start(ffw[:, n, :], w).then_inc(d_ffw[n], 16)
            sp.dma_start(ctx_sb[:], ctx[0]).then_inc(ctx_in, 16)

            def load_x(b):
                sp.wait_ge(sg["xn1"], b)
                sp.wait_ge(sg["xres"], b)
                src = x[b] if type(b) is int else x[bass.ds(b, 1)].rearrange("a p n -> (a p) n")
                sp.dma_start(x_sb[:], src).then_inc(x_in, 16)

            def load_ctx(b):
                sp.wait_ge(sg["xproj"], (b - 1) * 3 + 2)
                src = ctx[b] if type(b) is int else ctx[bass.ds(b, 1)].rearrange("a p n -> (a p) n")
                sp.dma_start(ctx_sb[:], src).then_inc(ctx_in, 16)

            def store(b):
                sp.wait_ge(sg["outt"], b + 1)
                dst = out[b] if type(b) is int else out[bass.ds(b, 1)].rearrange("a p n -> (a p) n")
                sp.dma_start(dst, outt[:]).then_inc(out_st, 16)
                sp.wait_ge(out_st, b * 16 + 16)
                sp.sem_inc(out_free, 1)

            load_x(2)
            load_ctx(1)
            with sp.Fori(2, B - 1) as i:
                load_x(i + 1)
                load_ctx(i)
                store(i - 2)
            load_ctx(B - 1)
            for b in range(B - 3, B):
                store(b)

        @block.tensor
        def _(pe):
            mm = nc.tensor.matmul

            def w_totals(_, n):
                pe.wait_ge(ones_set, 1)
                pe.wait_ge(ffsum, 4)
                mm(Bk[0][:, 0:4], ones[:], small[:, 0:4], start=True, stop=True).then_inc(totals, 1)

            def s_transpose_x(b, _):
                wait(pe, "xn1", b, 1)
                if not (type(b) is int and b == 0):
                    wait(pe, "masked", b - 1, NH - GRP)
                for k in range(KD):
                    last = nc.tensor.transpose(A[0][:, k * P:(k + 1) * P], xn1[:, k * P:(k + 1) * P], ident)
                last.then_inc(sg["xnT_ps"], 1)

            def s_qkv(b, n):
                if n == 0:
                    wait(pe, "xnTl", b, 1)
                elif n == 1:
                    wait(pe, "x1", b, 0)
                elif n == 2:
                    wait(pe, "oTl", b, 0)
                elif n == 3:
                    wait(pe, "rope_mul", b, 2)
                elif n == 4:
                    wait(pe, "v_sb", b, 1)
                elif n == 5:
                    wait(pe, "rope_mul", b, 4)
                pe.wait_ge(w_lo, n + 1)
                parts = [(k, a, w) for k in range(KD) for a, w in ((0, 0), (0, 1), (1, 0))]
                for k, a, w in parts:
                    last = mm(QB[n % 3], xnT[:, a, k, :], wqkv[:, w, n, k, :], start=((k, a, w) == parts[0]), stop=((k, a, w) == parts[-1]))
                last.then_inc(sg["qkv_ps"], 1)

            def s_transpose(b, n):
                if n < 2:
                    wait(pe, "kswap", b, 1)
                    src = [ks[:, g, v] for g in range(4 * n, 4 * n + 4) for v in range(2)]
                else:
                    wait(pe, "lo", b, n)
                    src = [qs[:, n % 2, h] for h in range(8)]
                wait(pe, "qkT", b, n) if n else wait(pe, "pT", b, 0)
                dst = A[2].bitcast(F16)
                for m, a in enumerate(src):
                    last = nc.tensor.transpose(dst[:, m * P:(m + 1) * P], a.rearrange("p t d -> p (t d)"), ident16)
                last.then_inc(sg["qkT_ps"], 1)

            def s_scores(b, g):
                wait(pe, "qkT", b, 3 + g // 2)
                if g >= 2:
                    wait(pe, "masked", b, 4 * (g - 1))
                else:
                    wait(pe, "rope_mul", b, 6 + 2 * g)
                for j in range(GRP):
                    for v in range(2):
                        last = mm(A[g % 2][:, j * P:(j + 1) * P], qT[:, GRP * g + j, :], kT[:, g, v, :],
                                  start=(v == 0), stop=(v == 1))
                last.then_inc(sg["s_ps"], 1)

            def s_transpose_p(b, g):
                wait(pe, "normed", b, g + 1)
                wait(pe, "pT", b, g) if g else wait(pe, "qkT", b, 6)
                for j in range(GRP):
                    last = nc.tensor.transpose(A[2][:, j * P:(j + 1) * P], ex[:, g % 2, j, :], ident)
                last.then_inc(sg["pT_ps"], 1)

            def s_pv(b, g):
                if g == 0:
                    wait(pe, "v_sb", b, 1)
                    wait(pe, "rope_mul", b, 10)
                if g % 2 == 0 and g:
                    wait(pe, "oTl", b, g // 2)
                wait(pe, "pT", b, g + 1)
                e = g % 2
                mm(A[3][HD * e:HD * e + HD, :], v_sb[:, g * HD:(g + 1) * HD], pT[:, g % 2, :],
                   start=True, stop=True).then_inc(sg["pv"], 1)

            def s_wo(b, n):
                if n == 0:
                    wait(pe, "masked", b, NH)
                wait(pe, "oTl", b, n + 1)
                pe.wait_ge(wo_lo, n // 2 + 1)
                for j in range(GRP):
                    for m, (a, w) in enumerate(((0, 0), (0, 1), (1, 0))):
                        last = mm(A[1][:, 0:D], oT[:, a, n, j, :], wo[:, w, n, j, :], start=(n == 0 and j == 0 and m == 0),
                                  stop=(n == NPAIR - 1 and j == GRP - 1 and m == 2))
                if n == NPAIR - 1:
                    last.then_inc(sg["o_ps"], 1)

            def k_proj_k(b, _):
                pe.wait_ge(d_x, 32)
                pe.wait_ge(ctx_in, b * 16 + 16)
                if kb(b) is A:
                    wait(pe, "x1", b, 1)
                else:
                    wait(pe, "x2", b, 0)
                for m in range(2):
                    last = mm(kb(b)[0][:, m * T:(m + 1) * T], xw_sb[:, 2 + m, :], ctx_sb[:], start=True, stop=True)
                last.then_inc(sg["xproj"], 1)

            def k_proj_v(b, _):
                for m in range(TB):
                    last = mm(v_bank(b)[:, m * P:(m + 1) * P], ctx_sb[:, m * P:(m + 1) * P], xw_sb[:, 4, :], start=True, stop=True)
                last.then_inc(sg["xproj"], 1)

            def k_proj_q(b, _):
                wait(pe, "xn2", b, 1)
                if kb(b) is Bk:
                    wait(pe, "xv", b, 1)
                for m in range(2):
                    last = mm(kb(b)[1][:, m * T:(m + 1) * T], xw_sb[:, m, :], xn2[:], start=True, stop=True)
                last.then_inc(sg["xproj"], 1)

            def k_spread(b, n):
                wait(pe, "xr_lo", b, n // 2 + 1)
                if n == 1:
                    wait(pe, "xr_mul", b, 4)
                elif n >= 2:
                    wait(pe, "kst", b, n - 1)
                for q in range(2):
                    hg = 2 * (n % 2) + q
                    for v, name in enumerate((("k_hi", "k_lo"), ("q_hi", "q_lo"))[n // 2]):
                        at = C16[name][0] + hg * P
                        last = mm(kb(b)[n % 2][:, q * T:(q + 1) * T], k16[:, at:at + P], xhl[:, n // 2, v, :], start=(v == 0), stop=(v == 1))
                last.then_inc(sg["sel_ps"], 1)

            hidden = {}

            def masked(dst, pairs, stop):
                mm(dst, bigi[:, 0, :], pairs, start=False, stop=False)
                mm(dst, bigi[:, 1, :], pairs, start=False, stop=False)
                return mm(dst, k16[:, P:2 * P], pairs, start=False, stop=stop)

            def k_scores(b, h):
                if h == 0:
                    wait(pe, "kz", b, XJ)
                    wait(pe, "qst", b, 2)
                elif 2 <= h < 6:
                    wait(pe, "xmax", b, h - 1)
                elif h >= 8:
                    wait(pe, "xmax", b, h - 3)
                elif h == 6 and kb(b) is Bk:
                    wait(pe, "outt", b, 0)
                elif h == 6:
                    wait(pe, "xv", b, 1)

                def products(hide):
                    for m in range(TB):
                        dst = scores_bank(b, h)[:, m * T:(m + 1) * T]
                        last = mm(dst, qst[:, h // XJ, m * P:(m + 1) * P], kz[:, h // XJ, h % XJ, :], start=True, stop=not hide)
                        if hide:
                            last = masked(dst, nbn[:, m, :], True)
                    last.then_inc(sg["nat_ps"], 1)

                with pe.If(hidden["any"]):
                    products(True)
                with pe.Else():
                    products(False)

            def k_max_transpose(b, _):
                wait(pe, "mt", b, 1)
                dst = kb(b)[2].bitcast(F16)
                for hg in range(XG):
                    for m in range(TB):
                        last = nc.tensor.transpose(dst[:, hg * T + m * P:hg * T + (m + 1) * P], mt[:, m, hg, :], ident16)
                last.then_inc(sg["mt_ps"], 1)

            def c_transposed(b, h):
                if h == 0:
                    if type(b) is int:
                        wait(pe, "outt", b, 0)
                    wait(pe, "qaug", b, 1)
                elif h >= 2:
                    wait(pe, "xexp", b, h - 1)

                def products(hide):
                    for m in range(TB):
                        dst = Bk[2 + h % 2][:, m * T:(m + 1) * T]
                        k = kz[:, h // XJ, h % XJ, m * P:(m + 1) * P]
                        if hide:
                            mm(dst, k, qst[:, h // XJ, :], start=True, stop=False)
                            masked(dst, nbt[:, m, :], False)
                            last = mm(dst, k, mrow[:, h // XJ, :], start=False, stop=True)
                        else:
                            last = mm(dst, k, qaug[:, h // XJ, :], start=True, stop=True)
                    last.then_inc(sg["st_ps"], 1)

                with pe.If(hidden["any"]):
                    products(True)
                with pe.Else():
                    products(False)

            def c_pv(b, h):
                hg, j = h // XJ, h % XJ
                wait(pe, "xexp", b, h + 1)
                if j == 0 and hg >= 2:
                    wait(pe, "bc", b, hg - 1)
                for m in range(TB):
                    last = mm(Bk[hg % 2][32 * j:32 * j + 32, 0:T], vaug[:, m, h, :], xpT[:, h % 2, m, :],
                              start=(m == 0), stop=(m == TB - 1))
                last.then_inc(sg["xpv"], 1)

            def c_sums(b, hg):
                wait(pe, "oraw", b, hg + 1)
                mm(Bk[hg % 2][:, T:2 * T], c("selsum"), oraw[:, hg, :], start=True, stop=True).then_inc(sg["bc_ps"], 1)

            def c_wo(b, _):
                wait(pe, "onorm", b, XG)
                for hg in range(XG):
                    last = mm(Bk[0][:, 0:T], xwo_sb[:, hg, :], oraw[:, hg, :], start=(hg == 0), stop=(hg == XG - 1))
                last.then_inc(sg["wo_ps"], 1)

            def f_transpose_x(b, _):
                wait(pe, "xn3", b, 1)
                for k in range(KD):
                    last = nc.tensor.transpose(Bk[3][:, k * P:(k + 1) * P], xn3[:, k * P:(k + 1) * P], ident)
                last.then_inc(sg["x3T_ps"], 1)

            def f_up_gate(b, n):
                if n == 0:
                    wait(pe, "x3l", b, 1)
                elif n >= 2:
                    wait(pe, "fhid", b, n - 1)
                for w in range(2):
                    for e in range(2):
                        at = (2 * n + e) * P
                        for m in range(2 * KD):
                            k, v = m // 2, m % 2
                            last = mm(Bk[2 + n % 2][:, (2 * w + e) * P:(2 * w + e + 1) * P], tern[:, w, k * E + at:k * E + at + P],
                                      x3[:, v, k, :], start=(m == 0), stop=(m == 2 * KD - 1))
                last.then_inc(sg["ff_ps"], 1)

            def f_down(b, _):
                wait(pe, "fl", b, NF)
                for e in range(ET):
                    for v in range(2):
                        last = mm(Bk[2][:, 0:D], hid[:, v, e, :], tern[:, 2, e * D:(e + 1) * D],
                                  start=(e == 0 and v == 0), stop=(e == ET - 1 and v == 1))
                last.then_inc(sg["dn_ps"], 1)

            steps = dict(
                S=dict(transpose_x=s_transpose_x, qkv=s_qkv, transpose=s_transpose, scores=s_scores, transpose_p=s_transpose_p,
                       pv=s_pv, wo=s_wo),
                K=dict(proj_k=k_proj_k, proj_v=k_proj_v, proj_q=k_proj_q, spread=k_spread, scores=k_scores,
                       max_transpose=k_max_transpose),
                C=dict(transposed=c_transposed, pv=c_pv, sums=c_sums, wo=c_wo),
                F=dict(transpose_x=f_transpose_x, up_gate=f_up_gate, down=f_down),
                W=dict(totals=w_totals))
            pe.wait_ge(d_first, 32)
            run(steps, FIRST, S=0, W=0, Q=1)
            pe.wait_ge(flagged, 1)
            pe.wait_ge(terns, 3)
            pe.wait_ge(zeroed, 4)
            pe.wait_ge(d_const, 32)
            hidden["any"] = pe.value_load(flag[0:1, 0:1])
            rounds(pe, steps)

        @block.vector
        def _(dve):
            v = nc.vector

            def ln_stats(b, src, stt, mv, n):
                ln = f"ln{n}"
                v.bn_stats(stt[:], src[:]).then_inc(sg[ln], 1)
                wait(dve, ln, b, 1)
                dve.sem_inc(passed, 1)
                v.bn_aggr(mv[:, 0:2], stt[:]).then_inc(sg[ln], 1)
                wait(dve, ln, b, 2)
                v.tensor_scalar(mv[:, 2:3], mv[:, 1:2], EPS_LN, None, ALU.add).then_inc(sg[ln], 1)

            def ln_apply(b, src, mv, rs, dst, n):
                wait(dve, f"rstd{n}", b, 1)
                v.tensor_scalar(dst[:], src[:], mv[:, 0:1], rs[:], ALU.subtract, ALU.mult).then_inc(sg[f"xn{n}"], 1)

            def s_ln_stats(b, _):
                dve.wait_ge(x_in, b * 16 + 16)
                ln_stats(b, x_sb, st1, mv1, 1)

            def s_v_out(b, _):
                wait(dve, "qkv_ps", b, 2)
                v.scalar_tensor_tensor(out=v_sb[:], in0=QB[1], scalar=1.0 / WS, in1=rowb[:, R_V:R_V + 512],
                                       op0=ALU.mult, op1=ALU.add).then_inc(sg["v_sb"], 1)

            def s_low_xn(b, _):
                wait(dve, "xnT", b, 1)
                v.tensor_tensor(xnT[:, 1], A[0][:, 0:D].rearrange("p (k s) -> p k s", k=KD), xnT[:, 0], ALU.subtract).then_inc(sg["xnTl"], 1)

            def s_rope(b, r):
                n = r + 1 if r else 0
                wait(dve, "qkv_ps", b, n + 1)
                wait(dve, "lo", b, max(0, r - 1))
                for to, x, by in factors(r, QB[n % 3], rot[:, r % 2, :], rot_b[:, r % 2, :]):
                    v.tensor_tensor(to, x, by, ALU.mult).then_inc(sg["rope_mul"], 1)

            def s_low(b, r):
                if r == 0:
                    wait(dve, "hi", b, 1)
                    low_part(v, 0).then_inc(sg["lo"], 1)
                    wait(dve, "lo", b, 1)
                    v.tensor_copy(ks[:, :, 1], ks[:, :, 0, ::-1, :]).then_inc(sg["kswap"], 1)

            def s_mask(b, g):
                wait(dve, "s_ps", b, g + 1)
                if g >= 2:
                    wait(dve, "expd", b, 4 * (g - 1))
                dve.sem_inc(passed, 1)
                for j in range(GRP):
                    h = GRP * g + j
                    v.tensor_tensor_reduce(out=sm[:, g % 2, j, :], in0=A[g % 2][:, j * P:(j + 1) * P], in1=c("causal"),
                                           scale=1.0, scalar=3.0e38, op0=ALU.add, op1=ALU.min,
                                           accum_out=nmax[:, h:h + 1]).then_inc(sg["masked"], 1)

            def s_recip(b, g):
                wait(dve, "expd", b, GRP * (g + 1))
                v.reciprocal(rinv[:, GRP * g:GRP * (g + 1)], ssum[:, GRP * g:GRP * (g + 1)]).then_inc(sg["rsum"], 1)

            def s_x1_out(b, _):
                wait(dve, "o_ps", b, 1)
                wait(dve, "xres", b, 1)
                wait(dve, "x1r", b, 0)
                v.scalar_tensor_tensor(out=x1[:], in0=A[1][:, 0:D], scalar=1.0 / WS, in1=xres[:],
                                       op0=ALU.mult, op1=ALU.add).then_inc(sg["x1"], 1)

            def s_low_o(b, n):
                wait(dve, "oT", b, n + 1)
                hi, lo = (oT[:, w, n].rearrange("p j s -> p (j s)") for w in range(2))
                v.tensor_tensor(lo, A[3], hi, ALU.subtract).then_inc(sg["oTl"], 1)

            def k_ln_stats(b, _):
                wait(dve, "x1", b, 1)
                ln_stats(b, x1, st2, mv2, 2)

            def rope_cross(b, n):
                bias = 2 * (1 - n)
                tab = ("xk_cos", "xk_sin") if n == 0 else ("xq_cos", "xq_sin")
                wait(dve, "xproj", b, (1, 3)[n])
                if n:
                    wait(dve, "xr_sum", b, 1)
                for m, dst in enumerate((xr_a, xr_b)):
                    v.scalar_tensor_tensor(out=dst[:], in0=kb(b)[n][:, m * T:(m + 1) * T], scalar=colb[:, bias + m:bias + m + 1],
                                           in1=c(tab[m]), op0=ALU.add, op1=ALU.mult).then_inc(sg["xr_mul"], 1)
                wait(dve, "xr_mul", b, 2 * n + 2)
                v.tensor_tensor(xr[:, n, :], xr_a[:], xr_b[:], ALU.add).then_inc(sg["xr_sum"], 1)
                wait(dve, "xr_sum", b, n + 1)
                v.tensor_copy(xhl[:, n, 0, :], xr[:, n, :]).then_inc(sg["xr_hi"], 1)
                wait(dve, "xr_hi", b, n + 1)
                v.tensor_tensor(xhl[:, n, 1, :], xr[:, n, :], xhl[:, n, 0, :], ALU.subtract).then_inc(sg["xr_lo"], 1)

            def k_v_out(b, _):
                wait(dve, "xproj", b, 2)
                wait(dve, "xpv", b, 0)
                v.tensor_tensor(vaug[:, :, :, 0:XC], v_bank(b)[:, 0:TB * P].rearrange("p (m h c) -> p m h c", m=TB, c=XC),
                                rowb[:, R_XBV:R_XBV + P].rearrange("p (o h c) -> p o h c", o=1, c=XC).to_broadcast([P, TB, XH, XC]),
                                ALU.add).then_inc(sg["xv"], 1)

            def k_zero_k(b, _):
                wait(dve, "kst", b, 2)
                for j in range(XJ):
                    r = slice(32 * j, 32 * j + 32)
                    v.tensor_copy(kz[r, :, j, :], kst[r, :, :]).then_inc(sg["kz"], 1)

            def k_max(b, h):
                wait(dve, "nat_ps", b, h + 1)
                v.tensor_reduce(xnm[:, h // XJ, h % XJ, :], scores_bank(b, h).rearrange("p (m t) -> p m t", m=TB), AX.X,
                                ALU.min).then_inc(sg["xmax"], 1)

            def k_max_pack(b, _):
                wait(dve, "xmax", b, XH)
                for m in range(TB):
                    last = v.tensor_scalar(mt[:, m, :, :].rearrange("p g (j r) -> p g j r", r=32)[:, :, :, MROW], xnm[:, :, :, m],
                                           -1.0 / MSCALE, None, ALU.mult)
                last.then_inc(sg["mt"], 1)

            def k_add_max(b, _):
                wait(dve, "mrow", b, 1)
                v.tensor_tensor(qaug[:], qst[:], mrow[:], ALU.add).then_inc(sg["qaug"], 1)

            def c_recip(b, hg):
                wait(dve, "bc_ps", b, hg + 1)
                if hg >= 2:
                    wait(dve, "onorm", b, hg - 1)
                v.reciprocal(bcs[:, hg % 2, :], Bk[hg % 2][:, T:2 * T]).then_inc(sg["bc"], 1)

            def c_x2_out(b, _):
                wait(dve, "wo_ps", b, 1)
                wait(dve, "x1r", b, 1)
                v.tensor_tensor(x2[:], Bk[0][:, 0:T], x1r[:], ALU.add).then_inc(sg["x2"], 1)

            def f_ln_stats(b, _):
                wait(dve, "x2", b, 1)
                ln_stats(b, x2, st3, mv3, 3)

            def f_low_x(b, _):
                wait(dve, "x3h", b, 1)
                v.tensor_tensor(x3[:, 1], Bk[3][:, 0:D].rearrange("p (k s) -> p k s", k=KD), x3[:, 0], ALU.subtract).then_inc(sg["x3l"], 1)

            def f_act(b, n):
                u, g = Bk[2 + n % 2][:, 0:256], Bk[2 + n % 2][:, 256:512]
                wait(dve, "ftanh", b, n + 1)
                v.scalar_tensor_tensor(out=fe[:, n, :], in0=fe[:, n, :], scalar=1.0, in1=u, op0=ALU.add, op1=ALU.mult).then_inc(sg["fact"], 1)
                wait(dve, "fact", b, n + 1)
                v.scalar_tensor_tensor(out=fe[:, n, :], in0=fe[:, n, :], scalar=HS, in1=g, op0=ALU.mult, op1=ALU.mult).then_inc(sg["fhid"], 1)

            def f_low(b, n):
                wait(dve, "fh", b, n + 1)
                v.tensor_tensor(hid[:, 1, 2 * n:2 * n + 2, :], fe[:, n, :].rearrange("p (e s) -> p e s", s=P),
                                hid[:, 0, 2 * n:2 * n + 2, :], ALU.subtract).then_inc(sg["fl"], 1)

            def f_out(b, _):
                wait(dve, "dn_ps", b, 1)
                dve.wait_ge(out_free, b + 1)
                v.scalar_tensor_tensor(out=outt[:], in0=Bk[2][:, 0:D], scalar=small[:, 16:17], in1=x2[:],
                                       op0=ALU.mult, op1=ALU.add).then_inc(sg["outt"], 1)

            def w_turn(_, r):
                at = R_K if r == 0 else R_Q + 512 * (r - 1)
                if r == 0:
                    dve.wait_ge(d_first, 32)
                    dve.wait_ge(d_row1, 16)
                    a, b = (t[:].rearrange("p g t -> p (g t)").bitcast(F32) for t in (qaug, kst))
                else:
                    dve.wait_ge(d_row, 32)
                    a, b = kz[:, r - 1].rearrange("p j t -> p (j t)").bitcast(F32), oT[:, (r - 1) // 2, 2 * ((r - 1) % 2):2 * ((r - 1) % 2) + 2].rearrange("p n j s -> p (n j s)").bitcast(F32)
                for to, x, by in factors(r, rowb[:, at:at + 512], a, b):
                    v.tensor_tensor(to, x, by, ALU.mult).then_inc(turned, 1)
                dve.wait_ge(turned, 4 * r + 2)
                v.tensor_tensor(a, a, b, ALU.add).then_inc(turned, 1)
                dve.wait_ge(turned, 4 * r + 3)
                v.tensor_scalar(rowb[:, at:at + 512], a, WS, None, ALU.mult).then_inc(turned, 1)

            def w_low_w(_, n):
                dve.wait_ge(w_hi, n + 1)
                hi, lo = (wqkv[:, w, n].rearrange("p k n -> p (k n)") for w in range(2))
                v.scalar_tensor_tensor(out=lo, in0=stage[:, n, :], scalar=WS, in1=hi, op0=ALU.mult, op1=ALU.subtract).then_inc(w_lo, 1)

            def w_low_o(_, n):
                dve.wait_ge(wo_hi, n + 1)
                hi, lo = (wo[:, w, 2 * n:2 * n + 2].rearrange("p n j d -> p (n j d)") for w in range(2))
                v.scalar_tensor_tensor(out=lo, in0=ffw[:, n, :], scalar=WS, in1=hi, op0=ALU.mult, op1=ALU.subtract).then_inc(wo_lo, 1)

            def w_tables(_, n):
                dve.wait_ge(d_first, 32)
                dve.wait_ge(d_row1, 16)
                kw = rowb[:, R_KW:R_KW + NH].rearrange("p (h o) -> p h o", o=1).to_broadcast([P, NH, HD])
                for dst, name in ((cq, "cos"), (sq, "sin")):
                    tab = c(name).rearrange("p (o d) -> p o d", o=1).to_broadcast([P, NH, HD])
                    v.scalar_tensor_tensor(out=dst[:], in0=tab, scalar=-float(HD) ** -0.5, in1=kw,
                                           op0=ALU.mult, op1=ALU.mult).then_inc(tabs, 1)
                dve.wait_ge(tabs, 2)

            def w_masks(_, n):
                dve.wait_ge(d_mask, 32)
                v.tensor_scalar(nbn[:].rearrange("p m t -> p (m t)"), maskn, 0.0, None, ALU.is_equal).then_inc(nbs, 1)
                v.tensor_scalar(nbt[:].rearrange("p m t -> p (m t)"), maskt, 0.0, None, ALU.is_equal).then_inc(nbs, 1)
                for m, s in enumerate((HUGE, -HUGE)):
                    v.tensor_scalar(bigi[:, m, :], ident, s, None, ALU.mult).then_inc(nbs, 1)
                dve.wait_ge(nbs, 4)
                v.tensor_reduce(small[:, 3:4], nbn[:], AX.XY, ALU.max).then_inc(ffsum, 1)

            def w_scales(_, n):
                dve.wait_ge(totals, 1)
                v.tensor_scalar(small[:, 4:7], Bk[0][:, 0:3], 1.0 / (D * E), EPS_Q, ALU.mult, ALU.add).then_inc(scales, 1)
                v.tensor_copy(flag[:], Bk[0][:, 3:4]).then_inc(flagged, 1)
                dve.wait_ge(scales, 1)
                v.tensor_scalar(small[:, 8:11], small[:, 4:7], 0.5, None, ALU.mult).then_inc(scales, 1)
                v.tensor_scalar(small[:, 12:15], small[:, 4:7], -0.5, None, ALU.mult).then_inc(scales, 1)
                v.tensor_scalar(small[:, 18:19], small[:, 4:5], 0.5, None, ALU.mult).then_inc(scales, 1)
                v.tensor_tensor(small[:, 17:18], small[:, 4:5], small[:, 5:6], ALU.mult).then_inc(scales, 1)
                dve.wait_ge(scales, 5)
                v.scalar_tensor_tensor(out=small[:, 16:17], in0=small[:, 17:18], scalar=0.5 / HS, in1=small[:, 6:7],
                                       op0=ALU.mult, op1=ALU.mult).then_inc(scales, 1)

            def w_ternary(_, n):
                v.tensor_scalar(tern[:, n, :], ffw[:, n, :], small[:, 12 + n:13 + n], None, ALU.is_lt).then_inc(scales, 1)
                dve.wait_ge(scales, 7 + n)
                v.scalar_tensor_tensor(out=tern[:, n, :], in0=ffw[:, n, :], scalar=small[:, 8 + n:9 + n], in1=tern[:, n, :],
                                       op0=ALU.is_gt, op1=ALU.subtract).then_inc(terns, 1)

            v.memset(ones[:], 1.0).then_inc(ones_set, 1)
            v.memset(half[:], -0.5).then_inc(pool_set, 1)
            steps = dict(
                S=dict(ln_stats=s_ln_stats, ln_apply=lambda b, _: ln_apply(b, x_sb, mv1, rs1, xn1, 1), rope=s_rope, v_out=s_v_out, low_xn=s_low_xn, low_o=s_low_o,
                       low=s_low, mask=s_mask, recip=s_recip, x1_out=s_x1_out),
                K=dict(ln_stats=k_ln_stats, ln_apply=lambda b, _: ln_apply(b, x1, mv2, rs2, xn2, 2),
                       rope_k=lambda b, _: rope_cross(b, 0), rope_q=lambda b, _: rope_cross(b, 1), v_out=k_v_out, zero_k=k_zero_k,
                       max=k_max, max_pack=k_max_pack, add_max=k_add_max),
                C=dict(recip=c_recip, x2_out=c_x2_out),
                F=dict(ln_stats=f_ln_stats, ln_apply=lambda b, _: ln_apply(b, x2, mv3, rs3, xn3, 3), low_x=f_low_x, act=f_act,
                       low=f_low, out=f_out),
                W=dict(low_w=w_low_w, low_o=w_low_o, tables=w_tables, turn=w_turn, masks=w_masks, scales=w_scales, ternary=w_ternary))
            run(steps, FIRST, S=0, W=0, Q=1)
            dve.wait_ge(terns, 3)
            dve.wait_ge(zeroed, 4)
            dve.wait_ge(d_const, 32)
            dve.wait_ge(d_row, 32)
            rounds(dve, steps)

        @block.scalar
        def _(act):
            a = nc.scalar
            act.dma_start(rowb[:, 0:R_Q], rows[:, 0:R_Q].to_broadcast([P, R_Q])).then_inc(d_row1, 16)
            act.dma_start(k16[:, 0:2 * P], c16[:, 0:2 * P]).then_inc(d_first, 16)
            act.dma_start(rowb[:, R_Q:], rows[:, R_Q:].to_broadcast([P, WROW - R_Q])).then_inc(d_row, 16)
            act.dma_start(colb[:], cols).then_inc(d_row, 16)
            act.dma_start(maskn, mask_n).then_inc(d_mask, 16)
            act.dma_start(maskt, mask_t).then_inc(d_mask, 16)
            act.dma_start(k32[:, W32_FIRST:], c32[:, W32_FIRST:]).then_inc(d_const, 16)
            act.dma_start(k16[:, 2 * P:], c16[:, 2 * P:]).then_inc(d_const, 16)
            act.dma_start(xw_sb[:], xw).then_inc(d_x, 16)
            act.dma_start(xwo_sb[:], xwo).then_inc(d_x, 16)

            def w_high_w(_, n):
                act.wait_ge(d_w[n], 16)
                a.activation(wqkv[:, 0, n].rearrange("p k n -> p (k n)"), stage[:, n, :], ACT.Identity, scale=WS).then_inc(w_hi, 1)

            def w_high_o(_, n):
                act.wait_ge(d_wo[n], 16)
                a.activation(wo[:, 0, 2 * n:2 * n + 2].rearrange("p n j d -> p (n j d)"), ffw[:, n, :], ACT.Identity, scale=WS).then_inc(wo_hi, 1)

            def w_sums(_, n):
                act.wait_ge(d_ffw[n], 16)
                a.activation(tern[:, n, :], ffw[:, n, :], ACT.Abs, accum_out=small[:, n:n + 1]).then_inc(ffsum, 1)

            def s_transpose_x(b, _):
                wait(act, "xnT_ps", b, 1)
                a.copy(xnT[:, 0], A[0][:, 0:D].rearrange("p (k s) -> p k s", k=KD)).then_inc(sg["xnT"], 1)

            def s_high(b, r):
                wait(act, "roped", b, r + 1)
                dst = ks[:, :, 0] if r == 0 else qs[:, (r - 1) % 2]
                if r >= 3:
                    wait(act, "qkT_ps", b, r)
                a.copy(dst[:, :, 0, :], rot[:, r % 2, :].rearrange("p (h d) -> p h d", d=HD)).then_inc(sg["hi"], 1)

            def s_transpose(b, n):
                wait(act, "qkT_ps", b, n + 1)
                dst = kT[:, 4 * n:4 * n + 4].rearrange("p g v s -> p (g v s)") if n < 2 else \
                    qT[:, 8 * (n - 2):8 * (n - 1)].rearrange("p h s -> p (h s)")
                a.copy(dst, A[2].bitcast(F16)).then_inc(sg["qkT"], 1)

            def s_exp(b, g):
                if g >= 2:
                    wait(act, "pT_ps", b, g - 1)
                for j in range(GRP):
                    h = GRP * g + j
                    wait(act, "masked", b, h + 1)
                    a.activation(ex[:, g % 2, j, :], sm[:, g % 2, j, :], ACT.Exp, bias=nmax[:, h:h + 1], scale=-1.0,
                                 accum_out=ssum[:, h:h + 1]).then_inc(sg["expd"], 1)

            def s_copy_p(b, g):
                wait(act, "pT_ps", b, g + 1)
                if g >= 2:
                    wait(act, "pv", b, g - 1)
                a.copy(pT[:, g % 2, :], A[2]).then_inc(sg["pT"], 1)

            def s_o_out(b, n):
                wait(act, "pv", b, 2 * n + 2)
                a.copy(oT[:, 0, n].rearrange("p j s -> p (j s)"), A[3]).then_inc(sg["oT"], 1)

            def k_spread(b, n):
                wait(act, "sel_ps", b, n + 1)
                wait(act, "xpv", b, 0)
                m = n % 2
                dst = (kst, qst)[n // 2][:, 2 * m:2 * m + 2, :].rearrange("p g t -> p (g t)")
                if n < 2:
                    a.activation(dst, kb(b)[m], ACT.Identity, bias=c("kcol")).then_inc(sg["kst"], 1)
                else:
                    a.copy(dst, kb(b)[m]).then_inc(sg["qst"], 1)

            def k_max_transpose(b, _):
                wait(act, "mt_ps", b, 1)
                a.copy(mrow[:].rearrange("p g t -> p (g t)"), kb(b)[2].bitcast(F16)).then_inc(sg["mrow"], 1)

            def c_exp(b, h):
                wait(act, "st_ps", b, h + 1)
                if h >= 2:
                    wait(act, "xpv", b, h - 1)
                a.activation(ffw[:, 0, 512 * (h % 2):512 * (h % 2) + 512], Bk[2 + h % 2], ACT.Exp, scale=-1.0).then_inc(sg["xexp"], 1)

            def c_out(b, hg):
                wait(act, "xpv", b, XJ * (hg + 1))
                a.copy(oraw[:, hg, :], Bk[hg % 2][:, 0:T]).then_inc(sg["oraw"], 1)

            def f_transpose_x(b, _):
                wait(act, "x3T_ps", b, 1)
                a.copy(x3[:, 0], Bk[3][:, 0:D].rearrange("p (k s) -> p k s", k=KD)).then_inc(sg["x3h"], 1)

            def f_tanh(b, n):
                wait(act, "ff_ps", b, n + 1)
                a.activation(fe[:, n, :], Bk[2 + n % 2][:, 0:256], ACT.Tanh, scale=small[:, 18:19]).then_inc(sg["ftanh"], 1)

            def f_high(b, n):
                wait(act, "fhid", b, n + 1)
                a.copy(hid[:, 0, 2 * n:2 * n + 2, :], fe[:, n, :].rearrange("p (e s) -> p e s", s=P)).then_inc(sg["fh"], 1)

            steps = dict(
                S=dict(transpose_x=s_transpose_x, high=s_high, transpose=s_transpose, exp=s_exp, copy_p=s_copy_p, o_out=s_o_out),
                K=dict(spread=k_spread, max_transpose=k_max_transpose),
                C=dict(exp=c_exp, out=c_out),
                F=dict(transpose_x=f_transpose_x, tanh=f_tanh, high=f_high),
                W=dict(high_w=w_high_w, high_o=w_high_o, sums=w_sums))
            run(steps, FIRST, S=0, W=0, Q=1)
            act.wait_ge(scales, 4)
            act.wait_ge(d_const, 32)
            rounds(act, steps)

        @block.gpsimd
        def _(pool):
            g_ = nc.gpsimd
            g_.memset(mt[:], 0.0).then_inc(zeroed, 1)
            g_.memset(vaug[:], 0.0).then_inc(zeroed, 1)
            pool.wait_ge(zeroed, 2)
            g_.memset(vaug[:, :, :, XC:2 * XC], 1.0).then_inc(zeroed, 1)
            pool.wait_ge(pool_set, 1)

            def power(b, mv, rs, n):
                wait(pool, f"ln{n}", b, 3)
                g_.tensor_tensor(rs[:], mv[:, 2:3], half[:], ALU.pow).then_inc(sg[f"rstd{n}"], 1)

            def s_ln_stats(b, _):
                power(b, mv1, rs1, 1)

            def s_keep_x(b, _):
                pool.wait_ge(x_in, b * 16 + 16)
                pool.wait_ge(d_row1, 16)
                wait(pool, "x1", b, 0)
                g_.tensor_tensor(xres[:], x_sb[:], rowb[:, R_BO:R_BO + D], ALU.add).then_inc(sg["xres"], 1)

            def s_bias(b, r):
                wait(pool, "rope_mul", b, 2 * r + 2)
                if type(b) is int and b == 0:
                    pool.wait_ge(turned, 4 * r + 4)
                at = R_K if r == 0 else R_Q + 512 * (r - 1)
                g_.tensor_tensor(rot_b[:, r % 2, :], rot_b[:, r % 2, :], rowb[:, at:at + 512], ALU.add).then_inc(sg["biased"], 1)
                wait(pool, "biased", b, r + 1)
                g_.tensor_tensor(rot[:, r % 2, :], rot[:, r % 2, :], rot_b[:, r % 2, :], ALU.add).then_inc(sg["roped"], 1)

            def s_low(b, r):
                if r:
                    wait(pool, "hi", b, r + 1)
                    wait(pool, "lo", b, r)
                    low_part(g_, r).then_inc(sg["lo"], 1)

            def s_recip(b, g):
                wait(pool, "rsum", b, g + 1)
                r = rinv[:, GRP * g:GRP * (g + 1)].rearrange("p (j o) -> p j o", o=1).to_broadcast([P, GRP, P])
                g_.tensor_tensor(ex[:, g % 2], ex[:, g % 2], r, ALU.mult).then_inc(sg["normed"], 1)

            def k_keep(b, _):
                wait(pool, "x1", b, 1)
                wait(pool, "x2", b, 0)
                g_.tensor_tensor(x1r[:], x1[:], colb[:, 4:5].to_broadcast([P, D]), ALU.add).then_inc(sg["x1r"], 1)

            def c_scale(b, hg):
                wait(pool, "bc", b, hg + 1)
                g_.tensor_tensor(oraw[:, hg, :], oraw[:, hg, :], bcs[:, hg % 2, :], ALU.mult).then_inc(sg["onorm"], 1)

            steps = dict(
                S=dict(ln_stats=s_ln_stats, keep_x=s_keep_x, bias=s_bias, low=s_low, recip=s_recip),
                K=dict(ln_stats=lambda b, _: power(b, mv2, rs2, 2), keep=k_keep),
                C=dict(scale=c_scale),
                F=dict(ln_stats=lambda b, _: power(b, mv3, rs3, 3)),
                W={})
            run(steps, FIRST, S=0, W=0, Q=1)
            pool.wait_ge(turned, 20)
            g_.memset(kz[:], 0.0).then_inc(zeroed, 1)
            pool.wait_ge(terns, 3)
            rounds(pool, steps)


def constants():
    f = np.float32
    c32 = np.zeros((P, W32), f)

    def put(name, a):
        c32[:, C32[name][0]:C32[name][1]] = a

    put("ident", np.eye(P, dtype=f))
    s = np.arange(P)
    put("causal", np.where(s[None, :] > s[:, None], f(BIG), f(0)))
    inv = (f(1) / f(10000.0) ** (np.arange(0, HD, 2, dtype=f) / f(HD))).astype(f)
    ang = np.arange(S, dtype=f)[:, None] * inv[None, :]
    put("cos", np.concatenate([np.cos(ang), np.cos(ang)], 1))
    put("sin", np.concatenate([-np.sin(ang), np.sin(ang)], 1))
    c32[:, C32["cos"][0]:C32["sin"][1]] /= f(WS)
    rd = XC // 2
    th = (f(1) / f(10000.0) ** (np.arange(0, rd, 2, dtype=f) / f(rd))).astype(f)
    ang = (np.arange(T, dtype=f)[:, None] * th[None, :]).T
    cosx, sinx = np.ones((XC, T), f), np.zeros((XC, T), f)
    cosx[0:2], cosx[2:4] = np.cos(ang), np.cos(ang)
    sinx[0:2], sinx[2:4] = -np.sin(ang), np.sin(ang)
    cosx, sinx = np.tile(cosx, (XH, 1)), np.tile(sinx, (XH, 1))
    put("xk_cos", cosx)
    put("xk_sin", sinx)
    scale = f(-1.0 / np.sqrt(XC))
    put("xq_cos", cosx * scale)
    put("xq_sin", sinx * scale)
    row = np.arange(P)
    put("kcol", np.where(row % 32 == MROW, f(MSCALE), f(0))[:, None])
    put("selsum", np.where(row[:, None] == 32 * (row[None, :] // 32) + XC, f(1), f(0)))
    c16 = np.zeros((P, W16), np.float16)
    c16[:, 0:P] = np.eye(P)
    c16[:, P:2 * P] = 10000.0 * np.eye(P)
    for name, slots in (("k_hi", (0, 2)), ("k_lo", (1,)), ("q_hi", (0, 1)), ("q_lo", (2,))):
        for hg in range(XG):
            for j in range(XJ):
                for r in slots:
                    for d in range(XC):
                        c16[(hg * XJ + j) * XC + d, C16[name][0] + hg * P + 32 * j + XC * r + d] = 1.0
    return c32, c16


def kernel(**inputs):
    import concourse.bacc as bacc
    from concourse.bass_utils import run_bass_kernel_spmd

    a = {k: np.asarray(v) for k, v in inputs.items()}

    def tiles(w):
        k, n = w.shape
        return w.reshape(k // P, P, n).transpose(1, 0, 2)

    wq, wk, wv = a["L0_attn_Wq"].T, a["L0_attn_Wk"].T, a["L0_attn_Wv"].T
    perm = np.arange(P).reshape(XH, XC)[:, [2, 3, 0, 1, 4, 5, 6, 7]].ravel()
    xwq, xwk, xwv = a["L0_xattn_wq"], a["L0_xattn_wk"], a["L0_xattn_wv"]
    xbq, xbk = a["L0_xattn_bq"], a["L0_xattn_bk"]
    xwo = np.zeros((XJ, 32, XG, P), np.float32)
    xwo[:, 0:XC] = a["L0_xattn_wo"].T.reshape(XG, XJ, XC, P).transpose(1, 2, 0, 3)
    mask = a["mask_1x1x2048x2048_if1"].reshape(T, T)
    c32, c16 = constants()
    arrays = dict(
        x=a["x"], ctx=a["ctx_2048"],
        mask_n=mask.reshape(TB, P, T).transpose(1, 0, 2).reshape(P, TB * T),
        mask_t=mask.T.reshape(TB, P, T).transpose(1, 0, 2).reshape(P, TB * T),
        w_qkv=tiles(np.concatenate([wk, wv, wq], 1)).reshape(P, KD, NCH, 512).transpose(0, 2, 1, 3).reshape(P, NCH, KD * 512),
        w_o=a["L0_attn_Wo"].T.reshape(NPAIR, 2, GRP, HD, D).transpose(1, 3, 0, 2, 4).reshape(P, 2, NPAIR // 2 * GRP * D),
        rows=np.concatenate([a["L0_attn_key_weights"], a["L0_attn_bk"], a["L0_attn_bv"], a["L0_attn_bo"], a["L0_attn_bq"],
                             a["L0_xattn_bv"]])[None],
        cols=np.stack([xbq, xbq[perm], xbk, xbk[perm], a["L0_xattn_bo"]], 1),
        xw=np.stack([xwq.T, xwq[perm].T, xwk.T, xwk[perm].T, xwv.T], 1),
        xwo=xwo.reshape(P, XG, P),
        w_up=tiles(a["L0_ffn_W_up"].T).reshape(P, KD * E),
        w_gate=tiles(a["L0_ffn_W_gate"].T).reshape(P, KD * E),
        w_down=tiles(a["L0_ffn_W_down"].T).reshape(P, ET * D),
        c32=c32, c16=c16)
    arrays = {k: np.ascontiguousarray(v) for k, v in arrays.items()}
    nc = bacc.Bacc("TRN2", target_bir_lowering=False, num_devices=1)
    aps = {k: nc.dram_tensor(f"in_{k}", v.shape, mybir.dt.from_np(v.dtype), kind="ExternalInput").ap() for k, v in arrays.items()}
    out = nc.dram_tensor("out_0", (B, S, D), F32, kind="ExternalOutput").ap()
    build(nc, *aps.values(), out)
    r = run_bass_kernel_spmd(nc, [{f"in_{k}": v for k, v in arrays.items()}], core_ids=[0])
    return r.results[0]["out_0"]
```
